# Optimizing a Trainium2 kernel written in Bass

```python
import numpy as np
import jax
import jax.numpy as jnp

def _softmax(x, axis=-1):
    return jax.nn.softmax(x, axis=axis)

def _gelu(x):
    return jax.nn.gelu(x, approximate=True)

def _silu(x):
    return jax.nn.silu(x)

def _sigmoid(x):
    return jax.nn.sigmoid(x)

def _layernorm(x, axis=-1, eps=1e-05):
    m = jnp.mean(x, axis=axis, keepdims=True)
    v = jnp.var(x, axis=axis, keepdims=True)
    return (x - m) / jnp.sqrt(v + eps)

def _scatter_add(tgt, idx, src, axis=0):
    return tgt.at[idx].add(src)

def _segment_sum(src, seg, n):
    return jax.ops.segment_sum(src, seg, n)
kernel_name = 'mk_decoder_preln_d2_seqx_r8_04154d'

def setup_inputs(seed: int=0):
    np.random.seed(seed)
    _w = jnp.asarray

    def _rec_inputs():
        import jax
        import jax.numpy as jnp
        _rk = jax.random.key(seed)
        x = 7.22e-05 + 1 * jax.random.normal(jax.random.fold_in(_rk, 1), (32, 56, 128), jnp.float32)
        _lenS = 56 - jax.random.randint(jax.random.fold_in(_rk, 7), (32,), 0, max(1, 56 // 4) + 1, jnp.int32)
        _lenS2 = 1500 - jax.random.randint(jax.random.fold_in(_rk, 8), (32,), 0, max(1, 1500 // 4) + 1, jnp.int32)
        _ctx_1024P = jax.random.normal(jax.random.fold_in(_rk, 11), (32, 16, 128), jnp.float32)
        _ctx_1024c = jax.random.dirichlet(jax.random.fold_in(_rk, 511), 0.3 * jnp.ones((16,), jnp.float32), (32, 1500))
        _ctx_1024t = jnp.einsum('bsk,bkd->bsd', _ctx_1024c, _ctx_1024P)
        _ctx_1024t = _ctx_1024t * jax.lax.rsqrt(jnp.mean(jnp.square(_ctx_1024t)) + 1e-12) * 0.953939
        ctx_1024 = 4.13588e-05 + 0.999923 * (_ctx_1024t + 0.3 * jax.random.normal(jax.random.fold_in(_rk, 611), (32, 1500, 128), jnp.float32))
        return (x, ctx_1024)
    x, ctx_1024 = _rec_inputs()

    def _L0_attn_setup():
        import jax, jax.numpy as jnp
        import numpy as np
        import math
        B, T, E, H = (2, 256, 128, 16)
        D = E // H

        def _l2norm(t):
            n = jnp.linalg.norm(t, axis=-1, keepdims=True)
            return t / jnp.maximum(n, 1e-12)
        key = jax.random.key(seed)
        ks = jax.random.split(key, 8)
        s = 1.0 / math.sqrt(E)
        x = jax.random.normal(ks[0], (B, T, E), dtype=jnp.float32)
        Wq = jax.random.normal(ks[1], (E, E), dtype=jnp.float32) * s
        Wk = jax.random.normal(ks[2], (E, E), dtype=jnp.float32) * s
        Wv = jax.random.normal(ks[3], (E, E), dtype=jnp.float32) * s
        Wa = jax.random.normal(ks[4], (E, H), dtype=jnp.float32) * s
        Wg = jax.random.normal(ks[5], (E, E), dtype=jnp.float32) * s
        Wo = jax.random.normal(ks[6], (E, E), dtype=jnp.float32) * s
        A_log = jnp.linspace(0.0, math.log(16.0), H, dtype=jnp.float32)
        dt_bias = jnp.zeros((H,), dtype=jnp.float32)
        rms_w = jnp.ones((D,), dtype=jnp.float32)
        return {'x': x, 'Wq': Wq, 'Wk': Wk, 'Wv': Wv, 'Wa': Wa, 'Wg': Wg, 'Wo': Wo, 'A_log': A_log, 'dt_bias': dt_bias, 'rms_w': rms_w}
    _L0_attn_all = _L0_attn_setup()
    _L0_attn_in = {k: v for k, v in _L0_attn_all.items() if k in ('Wq', 'Wk', 'Wv', 'Wa', 'Wg', 'Wo', 'A_log', 'dt_bias', 'rms_w')}
    del _L0_attn_all

    def _L0_xattn_setup():
        import jax, jax.numpy as jnp
        import numpy as np
        B, LQ, LK = (4, 256, 256)
        DQ, DK, DO = (128, 128, 128)
        key = jax.random.key(seed)
        ks = jax.random.split(key, 9)
        s = 0.02
        return {'query_input': jax.random.normal(ks[0], (B, LQ, DQ), jnp.float32), 'key_input': jax.random.normal(ks[1], (B, LK, DK), jnp.float32), 'value_input': jax.random.normal(ks[2], (B, LK, DK), jnp.float32), 'Wq': jax.random.normal(ks[3], (DQ, DO), jnp.float32) * s, 'bq': jax.random.normal(ks[4], (DO,), jnp.float32) * s, 'Wk': jax.random.normal(ks[5], (DK, DO), jnp.float32) * s, 'bk': jax.random.normal(ks[6], (DO,), jnp.float32) * s, 'Wv': jax.random.normal(ks[7], (DK, DO), jnp.float32) * s, 'bv': jax.random.normal(ks[8], (DO,), jnp.float32) * s}
    _L0_xattn_all = _L0_xattn_setup()
    _L0_xattn_in = {k: v for k, v in _L0_xattn_all.items() if k in ('Wq', 'bq', 'Wk', 'bk', 'Wv', 'bv')}
    del _L0_xattn_all

    def _L0_ffn_setup():
        import jax, jax.numpy as jnp
        import numpy as np
        B, L, D, E, K, DFF = (2, 256, 128, 8, 2, 512)
        key = jax.random.key(seed)
        kx, kr, kg, ku, kd = jax.random.split(key, 5)
        scale = 0.02
        return {'x': jax.random.normal(kx, (B, L, D), dtype=jnp.float32), 'Wr': jax.random.normal(kr, (E, D), dtype=jnp.float32) * scale, 'Wg': jax.random.normal(kg, (E, DFF, D), dtype=jnp.float32) * scale, 'Wu': jax.random.normal(ku, (E, DFF, D), dtype=jnp.float32) * scale, 'Wd': jax.random.normal(kd, (E, D, DFF), dtype=jnp.float32) * scale}
    _L0_ffn_all = _L0_ffn_setup()
    _L0_ffn_in = {k: v for k, v in _L0_ffn_all.items() if k in ('Wr', 'Wg', 'Wu', 'Wd')}
    del _L0_ffn_all

    def _L1_attn_setup():
        import math
        import jax, jax.numpy as jnp
        import numpy as np
        N_HEADS = 16
        ROPE_BASE = 10000.0

        def rotate_half(x):
            x_even = x[..., ::2]
            x_odd = x[..., 1::2]
            return jnp.stack((-x_odd, x_even), axis=-1).reshape(x.shape)

        def rope_cache(seq_len, head_dim, dtype):
            pos = jnp.arange(seq_len, dtype=jnp.float32)
            freqs = 1.0 / ROPE_BASE ** (jnp.arange(0, head_dim, 2, dtype=jnp.float32) / head_dim)
            angles = pos[:, None] * freqs[None, :]
            cos = jnp.repeat(jnp.cos(angles), 2, axis=-1).astype(dtype)
            sin = jnp.repeat(jnp.sin(angles), 2, axis=-1).astype(dtype)
            return (cos, sin)
        key = jax.random.key(seed)
        ks = jax.random.split(key, 5)
        B, S, D = (2, 256, 128)
        scale = 1.0 / math.sqrt(D)
        return {'x': jax.random.normal(ks[0], (B, S, D), dtype=jnp.float32), 'wq': jax.random.normal(ks[1], (D, D), dtype=jnp.float32) * scale, 'wk': jax.random.normal(ks[2], (D, D), dtype=jnp.float32) * scale, 'wv': jax.random.normal(ks[3], (D, D), dtype=jnp.float32) * scale, 'wo': jax.random.normal(ks[4], (D, D), dtype=jnp.float32) * scale}
    _L1_attn_all = _L1_attn_setup()
    _L1_attn_in = {k: v for k, v in _L1_attn_all.items() if k in ('wq', 'wk', 'wv', 'wo')}
    del _L1_attn_all

    def _L1_xattn_setup():
        import jax, jax.numpy as jnp
        import numpy as np
        D_MODEL = 128
        H = 16
        D_K = D_MODEL // H
        key = jax.random.key(seed)
        ks = jax.random.split(key, 11)
        B, S = (2, 256)
        scale = 1.0 / np.sqrt(D_MODEL)
        inp = {'query': jax.random.normal(ks[0], (B, S, D_MODEL), jnp.float32), 'key': jax.random.normal(ks[1], (B, S, D_MODEL), jnp.float32), 'value': jax.random.normal(ks[2], (B, S, D_MODEL), jnp.float32), 'Wq': jax.random.normal(ks[3], (D_MODEL, D_MODEL), jnp.float32) * scale, 'bq': jnp.zeros((D_MODEL,), jnp.float32), 'Wk': jax.random.normal(ks[4], (D_MODEL, D_MODEL), jnp.float32) * scale, 'bk': jnp.zeros((D_MODEL,), jnp.float32), 'Wv': jax.random.normal(ks[5], (D_MODEL, D_MODEL), jnp.float32) * scale, 'bv': jnp.zeros((D_MODEL,), jnp.float32), 'Wo': jax.random.normal(ks[6], (D_MODEL, D_MODEL), jnp.float32) * scale, 'bo': jnp.zeros((D_MODEL,), jnp.float32)}
        return inp
    _L1_xattn_all = _L1_xattn_setup()
    _L1_xattn_in = {k: v for k, v in _L1_xattn_all.items() if k in ('Wq', 'bq', 'Wk', 'bk', 'Wv', 'bv', 'Wo', 'bo')}
    del _L1_xattn_all

    def _L1_ffn_setup():
        import math
        import jax, jax.numpy as jnp
        import numpy as np
        H = 128
        F = 512
        E = 8
        TOP_K = 2
        CAP_FACTOR = 1.25
        MIN_CAP = 4
        SHARED_SCALE = 0.1

        def _top2_gating(logits, capacity):
            N, nE = logits.shape
            gates = jax.nn.softmax(logits, axis=-1)
            idx1 = jnp.argmax(gates, axis=-1)
            mask1 = jax.nn.one_hot(idx1, nE, dtype=gates.dtype)
            idx2 = jnp.argmax(gates * (1.0 - mask1), axis=-1)
            mask2 = jax.nn.one_hot(idx2, nE, dtype=gates.dtype)
            pos1 = jnp.cumsum(mask1, axis=0) - mask1
            mask1 = mask1 * (pos1 < capacity)
            pos2 = jnp.cumsum(mask2, axis=0) - mask2 + jnp.sum(mask1, axis=0, keepdims=True)
            mask2 = mask2 * (pos2 < capacity)
            g1 = jnp.sum(gates * mask1, axis=-1)
            g2 = jnp.sum(gates * mask2, axis=-1)
            denom = jnp.maximum(g1 + g2, jnp.finfo(gates.dtype).eps)
            g1, g2 = (g1 / denom, g2 / denom)
            loc1 = jnp.sum(pos1 * mask1, axis=-1).astype(jnp.int32)
            loc2 = jnp.sum(pos2 * mask2, axis=-1).astype(jnp.int32)
            oh1 = jax.nn.one_hot(loc1, capacity, dtype=gates.dtype)
            oh2 = jax.nn.one_hot(loc2, capacity, dtype=gates.dtype)
            combine = (g1[:, None] * mask1)[:, :, None] * oh1[:, None, :] + (g2[:, None] * mask2)[:, :, None] * oh2[:, None, :]
            dispatch = (combine > 0).astype(gates.dtype)
            return (combine, dispatch)
        key = jax.random.key(seed)
        ks = jax.random.split(key, 10)
        s_h = 1.0 / math.sqrt(H)
        s_f = 1.0 / math.sqrt(F)
        return {'hidden_states': jax.random.normal(ks[0], (2, 256, H), jnp.float32), 'router_w': jax.random.uniform(ks[1], (H, E), jnp.float32, -s_h, s_h), 'w1': jax.random.uniform(ks[2], (E, H, F), jnp.float32, -s_h, s_h), 'b1': jax.random.uniform(ks[3], (E, F), jnp.float32, -s_h, s_h), 'w2': jax.random.uniform(ks[4], (E, F, H), jnp.float32, -s_f, s_f), 'b2': jax.random.uniform(ks[5], (E, H), jnp.float32, -s_f, s_f), 'sw1': jax.random.uniform(ks[6], (H, F), jnp.float32, -s_h, s_h), 'sb1': jax.random.uniform(ks[7], (F,), jnp.float32, -s_h, s_h), 'sw2': jax.random.uniform(ks[8], (F, H), jnp.float32, -s_f, s_f), 'sb2': jax.random.uniform(ks[9], (H,), jnp.float32, -s_f, s_f)}
    _L1_ffn_all = _L1_ffn_setup()
    _L1_ffn_in = {k: v for k, v in _L1_ffn_all.items() if k in ('router_w', 'w1', 'b1', 'w2', 'b2', 'sw1', 'sb1', 'sw2', 'sb2')}
    del _L1_ffn_all
    return {'x': x, 'ctx_1024': ctx_1024, 'L0_attn_Wq': _L0_attn_in['Wq'], 'L0_attn_Wk': _L0_attn_in['Wk'], 'L0_attn_Wv': _L0_attn_in['Wv'], 'L0_attn_Wa': _L0_attn_in['Wa'], 'L0_attn_Wg': _L0_attn_in['Wg'], 'L0_attn_Wo': _L0_attn_in['Wo'], 'L0_attn_A_log': _L0_attn_in['A_log'], 'L0_attn_dt_bias': _L0_attn_in['dt_bias'], 'L0_attn_rms_w': _L0_attn_in['rms_w'], 'L0_xattn_Wq': _L0_xattn_in['Wq'], 'L0_xattn_bq': _L0_xattn_in['bq'], 'L0_xattn_Wk': _L0_xattn_in['Wk'], 'L0_xattn_bk': _L0_xattn_in['bk'], 'L0_xattn_Wv': _L0_xattn_in['Wv'], 'L0_xattn_bv': _L0_xattn_in['bv'], 'L0_ffn_Wr': _L0_ffn_in['Wr'], 'L0_ffn_Wg': _L0_ffn_in['Wg'], 'L0_ffn_Wu': _L0_ffn_in['Wu'], 'L0_ffn_Wd': _L0_ffn_in['Wd'], 'L1_attn_wq': _L1_attn_in['wq'], 'L1_attn_wk': _L1_attn_in['wk'], 'L1_attn_wv': _L1_attn_in['wv'], 'L1_attn_wo': _L1_attn_in['wo'], 'L1_xattn_Wq': _L1_xattn_in['Wq'], 'L1_xattn_bq': _L1_xattn_in['bq'], 'L1_xattn_Wk': _L1_xattn_in['Wk'], 'L1_xattn_bk': _L1_xattn_in['bk'], 'L1_xattn_Wv': _L1_xattn_in['Wv'], 'L1_xattn_bv': _L1_xattn_in['bv'], 'L1_xattn_Wo': _L1_xattn_in['Wo'], 'L1_xattn_bo': _L1_xattn_in['bo'], 'L1_ffn_router_w': _L1_ffn_in['router_w'], 'L1_ffn_w1': _L1_ffn_in['w1'], 'L1_ffn_b1': _L1_ffn_in['b1'], 'L1_ffn_w2': _L1_ffn_in['w2'], 'L1_ffn_b2': _L1_ffn_in['b2'], 'L1_ffn_sw1': _L1_ffn_in['sw1'], 'L1_ffn_sb1': _L1_ffn_in['sb1'], 'L1_ffn_sw2': _L1_ffn_in['sw2'], 'L1_ffn_sb2': _L1_ffn_in['sb2']}

def reference(x, ctx_1024, L0_attn_Wq, L0_attn_Wk, L0_attn_Wv, L0_attn_Wa, L0_attn_Wg, L0_attn_Wo, L0_attn_A_log, L0_attn_dt_bias, L0_attn_rms_w, L0_xattn_Wq, L0_xattn_bq, L0_xattn_Wk, L0_xattn_bk, L0_xattn_Wv, L0_xattn_bv, L0_ffn_Wr, L0_ffn_Wg, L0_ffn_Wu, L0_ffn_Wd, L1_attn_wq, L1_attn_wk, L1_attn_wv, L1_attn_wo, L1_xattn_Wq, L1_xattn_bq, L1_xattn_Wk, L1_xattn_bk, L1_xattn_Wv, L1_xattn_bv, L1_xattn_Wo, L1_xattn_bo, L1_ffn_router_w, L1_ffn_w1, L1_ffn_b1, L1_ffn_w2, L1_ffn_b2, L1_ffn_sw1, L1_ffn_sb1, L1_ffn_sw2, L1_ffn_sb2):
    import jax
    import jax.numpy as jnp

    def _L0_attn_ref(x, Wq, Wk, Wv, Wa, Wg, Wo, A_log, dt_bias, rms_w):
        import jax, jax.numpy as jnp
        import numpy as np
        import math
        B, T, E, H = (2, 256, 128, 16)
        D = E // H

        def _l2norm(t):
            n = jnp.linalg.norm(t, axis=-1, keepdims=True)
            return t / jnp.maximum(n, 1e-12)
        b, seq_len, e = x.shape
        h = A_log.shape[0]
        d = e // h
        q = _l2norm((x @ Wq).reshape(b, seq_len, h, d)).transpose(0, 2, 1, 3)
        k = _l2norm((x @ Wk).reshape(b, seq_len, h, d)).transpose(0, 2, 1, 3)
        v = (x @ Wv).reshape(b, seq_len, h, d).transpose(0, 2, 1, 3)
        dt = jax.nn.softplus(x @ Wa + dt_bias)
        alpha = jnp.exp(-jnp.exp(A_log) * dt)
        cum_log = jnp.cumsum(jnp.log(alpha + 1e-08), axis=1).transpose(0, 2, 1)
        log_l = cum_log[..., :, None] - cum_log[..., None, :]
        causal = jnp.tril(jnp.ones((seq_len, seq_len), dtype=bool))
        l_mat = jnp.where(causal, jnp.exp(log_l), 0.0)
        scores = jnp.einsum('bhid,bhjd->bhij', q, k) * l_mat
        out = jnp.einsum('bhij,bhjd->bhid', scores, v)
        out = out * jax.lax.rsqrt(jnp.mean(out * out, axis=-1, keepdims=True) + 1e-06) * rms_w
        out = out.transpose(0, 2, 1, 3).reshape(b, seq_len, e)
        gate = jax.nn.silu(x @ Wg)
        return out * gate @ Wo

    def _L0_xattn_ref(query_input, key_input, value_input, Wq, bq, Wk, bk, Wv, bv):
        import jax, jax.numpy as jnp
        import numpy as np
        B, LQ, LK = (4, 256, 256)
        DQ, DK, DO = (128, 128, 128)
        scale = jnp.asarray(DO, query_input.dtype) ** 0.5
        q = query_input @ Wq + bq
        k = key_input @ Wk + bk
        v = value_input @ Wv + bv
        attn = jnp.einsum('bqd,bkd->bqk', q, k) / scale
        attn = jax.nn.softmax(attn, axis=-1)
        return jnp.einsum('bqk,bkd->bqd', attn, v)

    def _L0_ffn_ref(x, Wr, Wg, Wu, Wd):
        import jax, jax.numpy as jnp
        import numpy as np
        B, L, D, E, K, DFF = (2, 256, 128, 8, 2, 512)
        Bb, Ll, Dd = x.shape
        T = Bb * Ll
        xt = x.reshape(T, Dd)
        logits = jnp.einsum('td,ed->te', xt, Wr)
        scores = jax.nn.softmax(logits, axis=-1)
        k_scores, k_ids = jax.lax.top_k(scores, K)
        eps = jnp.finfo(x.dtype).eps
        k_w = k_scores / (k_scores.sum(axis=-1, keepdims=True) + eps)
        combine = jnp.sum(jax.nn.one_hot(k_ids, E, dtype=x.dtype) * k_w[..., None], axis=1)
        g = jnp.einsum('td,efd->etf', xt, Wg)
        u = jnp.einsum('td,efd->etf', xt, Wu)
        h = jax.nn.relu(g) * u
        out_e = jnp.einsum('etf,edf->etd', h, Wd)
        out = jnp.einsum('te,etd->td', combine, out_e)
        return out.reshape(Bb, Ll, Dd)

    def _L1_attn_ref(x, wq, wk, wv, wo):
        import math
        import jax, jax.numpy as jnp
        import numpy as np
        N_HEADS = 16
        ROPE_BASE = 10000.0

        def rotate_half(x):
            x_even = x[..., ::2]
            x_odd = x[..., 1::2]
            return jnp.stack((-x_odd, x_even), axis=-1).reshape(x.shape)

        def rope_cache(seq_len, head_dim, dtype):
            pos = jnp.arange(seq_len, dtype=jnp.float32)
            freqs = 1.0 / ROPE_BASE ** (jnp.arange(0, head_dim, 2, dtype=jnp.float32) / head_dim)
            angles = pos[:, None] * freqs[None, :]
            cos = jnp.repeat(jnp.cos(angles), 2, axis=-1).astype(dtype)
            sin = jnp.repeat(jnp.sin(angles), 2, axis=-1).astype(dtype)
            return (cos, sin)
        B, S, D = x.shape
        H = N_HEADS
        hd = D // H

        def split_heads(t):
            return t.reshape(B, S, H, hd).transpose(0, 2, 1, 3)
        q = split_heads(x @ wq.T)
        k = split_heads(x @ wk.T)
        v = split_heads(x @ wv.T)
        cos, sin = rope_cache(S, hd, x.dtype)
        cos = cos[None, None]
        sin = sin[None, None]
        q = q * cos + rotate_half(q) * sin
        k = k * cos + rotate_half(k) * sin
        scores = jnp.einsum('bhqd,bhkd->bhqk', q, k) / math.sqrt(hd)
        causal_mask = jnp.triu(jnp.ones((S, S), dtype=bool), k=1)
        scores = jnp.where(causal_mask, jnp.finfo(scores.dtype).min, scores)
        pattern = jax.nn.softmax(scores, axis=-1)
        head_out = jnp.einsum('bhqk,bhkd->bhqd', pattern, v)
        merged = head_out.transpose(0, 2, 1, 3).reshape(B, S, D)
        out = merged @ wo.T
        return out

    def _L1_xattn_ref(query, key, value, Wq, bq, Wk, bk, Wv, bv, Wo, bo):
        import jax, jax.numpy as jnp
        import numpy as np
        D_MODEL = 128
        H = 16
        D_K = D_MODEL // H
        B, Sq, _ = query.shape

        def proj(x, W, b):
            y = x @ W.T + b
            return y.reshape(B, -1, H, D_K).transpose(0, 2, 1, 3)
        q = proj(query, Wq, bq)
        k = proj(key, Wk, bk)
        v = proj(value, Wv, bv)
        scores = jnp.einsum('bhqd,bhkd->bhqk', q, k) / jnp.sqrt(jnp.float32(D_K))
        attn = jax.nn.softmax(scores, axis=-1)
        ctx = jnp.einsum('bhqk,bhkd->bhqd', attn, v)
        ctx = ctx.transpose(0, 2, 1, 3).reshape(B, Sq, D_MODEL)
        return ctx @ Wo.T + bo

    def _L1_ffn_ref(hidden_states, router_w, w1, b1, w2, b2, sw1, sb1, sw2, sb2):
        import math
        import jax, jax.numpy as jnp
        import numpy as np
        H = 128
        F = 512
        E = 8
        TOP_K = 2
        CAP_FACTOR = 1.25
        MIN_CAP = 4
        SHARED_SCALE = 0.1

        def _top2_gating(logits, capacity):
            N, nE = logits.shape
            gates = jax.nn.softmax(logits, axis=-1)
            idx1 = jnp.argmax(gates, axis=-1)
            mask1 = jax.nn.one_hot(idx1, nE, dtype=gates.dtype)
            idx2 = jnp.argmax(gates * (1.0 - mask1), axis=-1)
            mask2 = jax.nn.one_hot(idx2, nE, dtype=gates.dtype)
            pos1 = jnp.cumsum(mask1, axis=0) - mask1
            mask1 = mask1 * (pos1 < capacity)
            pos2 = jnp.cumsum(mask2, axis=0) - mask2 + jnp.sum(mask1, axis=0, keepdims=True)
            mask2 = mask2 * (pos2 < capacity)
            g1 = jnp.sum(gates * mask1, axis=-1)
            g2 = jnp.sum(gates * mask2, axis=-1)
            denom = jnp.maximum(g1 + g2, jnp.finfo(gates.dtype).eps)
            g1, g2 = (g1 / denom, g2 / denom)
            loc1 = jnp.sum(pos1 * mask1, axis=-1).astype(jnp.int32)
            loc2 = jnp.sum(pos2 * mask2, axis=-1).astype(jnp.int32)
            oh1 = jax.nn.one_hot(loc1, capacity, dtype=gates.dtype)
            oh2 = jax.nn.one_hot(loc2, capacity, dtype=gates.dtype)
            combine = (g1[:, None] * mask1)[:, :, None] * oh1[:, None, :] + (g2[:, None] * mask2)[:, :, None] * oh2[:, None, :]
            dispatch = (combine > 0).astype(gates.dtype)
            return (combine, dispatch)
        B, S, h = hidden_states.shape
        x = hidden_states.reshape(-1, h)
        N = x.shape[0]
        capacity = min(max(MIN_CAP, math.ceil(TOP_K * CAP_FACTOR * N / E)), N)
        logits = x @ router_w
        combine, dispatch = _top2_gating(logits, capacity)
        expert_in = jnp.einsum('nec,nh->ech', dispatch, x)
        hmid = jax.nn.silu(jnp.einsum('ech,ehf->ecf', expert_in, w1) + b1[:, None, :])
        expert_out = jnp.einsum('ecf,efh->ech', hmid, w2) + b2[:, None, :]
        y = jnp.einsum('nec,ech->nh', combine, expert_out)
        shared = jax.nn.silu(x @ sw1 + sb1) @ sw2 + sb2
        out = y + SHARED_SCALE * shared
        return out.reshape(B, S, h)
    x = x + _L0_attn_ref(_layernorm(x, axis=-1), L0_attn_Wq, L0_attn_Wk, L0_attn_Wv, L0_attn_Wa, L0_attn_Wg, L0_attn_Wo, L0_attn_A_log, L0_attn_dt_bias, L0_attn_rms_w)
    x = x + _L0_xattn_ref(_layernorm(x, axis=-1), ctx_1024, ctx_1024, L0_xattn_Wq, L0_xattn_bq, L0_xattn_Wk, L0_xattn_bk, L0_xattn_Wv, L0_xattn_bv)
    x = x + _L0_ffn_ref(_layernorm(x, axis=-1), L0_ffn_Wr, L0_ffn_Wg, L0_ffn_Wu, L0_ffn_Wd)
    x = x + _L1_attn_ref(_layernorm(x, axis=-1), L1_attn_wq, L1_attn_wk, L1_attn_wv, L1_attn_wo)
    x = x + _L1_xattn_ref(_layernorm(x, axis=-1), ctx_1024, ctx_1024, L1_xattn_Wq, L1_xattn_bq, L1_xattn_Wk, L1_xattn_bk, L1_xattn_Wv, L1_xattn_bv, L1_xattn_Wo, L1_xattn_bo)
    x = x + _L1_ffn_ref(_layernorm(x, axis=-1), L1_ffn_router_w, L1_ffn_w1, L1_ffn_b1, L1_ffn_w2, L1_ffn_b2, L1_ffn_sw1, L1_ffn_sb1, L1_ffn_sw2, L1_ffn_sb2)
    return x

_drawn_inputs = setup_inputs


def setup_inputs(seed=0):
    import zlib

    import numpy as np

    out = dict(_drawn_inputs(seed))
    spreads = {'L0_attn_dt_bias': (0.0, 0.492),
     'L0_attn_rms_w': (1.0, 0.2),
     'L1_xattn_bq': (0.0, 0.388),
     'L1_xattn_bk': (0.0, 2.0),
     'L1_xattn_bv': (0.0, 0.1),
     'L1_xattn_bo': (0.0, 0.1)}
    factors = {'L0_xattn_Wq': 8.0,
     'L0_xattn_bq': 8.0,
     'L0_xattn_Wk': 8.0,
     'L0_xattn_bk': 64.0,
     'L0_ffn_Wr': 5.135,
     'L0_ffn_Wg': 5.412,
     'L0_ffn_Wu': 4.504,
     'L0_ffn_Wd': 4.372,
     'L1_ffn_b1': 6.111,
     'L1_ffn_b2': 4.072,
     'L1_ffn_sw1': 4.32,
     'L1_ffn_sb1': 8.0,
     'L1_ffn_sw2': 4.178,
     'L1_ffn_sb2': 39.557}
    for name, (base, spread) in spreads.items():
        noise = np.random.default_rng([zlib.crc32(name.encode()), seed]).standard_normal(out[name].shape)
        drawn = base * np.exp(spread * noise) if base else spread * noise
        out[name] = jnp.asarray(drawn.astype(out[name].dtype))
    for name, factor in factors.items():
        out[name] = (out[name] * factor).astype(out[name].dtype)
    return out
```

```python
from contextlib import ExitStack

import numpy as np

import concourse.bass as bass
from concourse import mybir

F32 = mybir.dt.float32
F32R = mybir.dt.float32r
ALU = mybir.AluOpType
ACT = mybir.ActivationFunctionType
AX_X = mybir.AxisListType.X

B, L, D = 32, 56, 128
NT = B * L
S = 1500
H, DH = 16, 8
G, HG = 4, 4
CH = 4
CW = NT // CH
PAIRS = B // 2
ST, SW = 12, S // 12
SB = 500
E, F = 8, 512
FT = F // 128
TT = NT // 128
CAPACITY = min(max(4, -(-2 * 5 * NT // (4 * E))), NT)
EPS_LN = 1e-5
EPS32 = float(np.finfo(np.float32).eps)
HIDE = -1e30


def constants():
    p = np.arange(128)
    out = {}
    out["ident"] = np.eye(128)
    out["mean"] = np.full((128, 128), 1.0 / D)
    out["head_sum"] = (p[:, None] // DH == p[None] // DH) * 1.0
    out["head_mean"] = out["head_sum"] / DH
    out["ones"] = np.ones((128, 128))
    out["before"] = (p[:, None] < p[None]) * 1.0
    same = p[:, None] // 64 == p[None] // 64
    out["after"] = (same & (p[:, None] > p[None])) * 1.0
    i = np.arange(L)
    real = (p % 64 < L)[:, None]
    out["upto"] = (real & (p[:, None] % 64 <= i[None])) * 1.0
    out["hide"] = np.where(i[None] <= p[:, None] % 64, 0.0, HIDE)
    out["diag"] = (real & (p[:, None] % 64 == i[None])) * 1.0
    out["head_of"] = (p[:, None] // DH == np.arange(H)[None]) * 1.0
    out["head_in_group"] = (p[:, None] % 32 // DH == np.arange(HG)[None]) * 1.0
    pos = np.arange(L, dtype=np.float32)
    freqs = (1.0 / np.float32(10000.0) ** (np.arange(0, DH, 2, dtype=np.float32) / np.float32(DH))).astype(np.float32)
    ang = pos[:, None] * freqs[None]
    out["cos"] = np.tile(np.repeat(np.cos(ang), 2, axis=1).T, (H, 1))
    out["sin"] = np.tile(np.repeat(np.sin(ang), 2, axis=1).T, (H, 1))
    out["rank"] = np.tile(float(E) - np.arange(E), (128, 1))
    nine = p % 32
    out["head_of_three"] = ((nine[:, None] // 9 == np.arange(3)[None]) & (nine[:, None] < 27)) * 1.0
    of = np.where(nine < 27, nine // 9, 0)
    out["spread_sum"] = ((p[:, None] // 32 == p[None] // 32) & (nine[:, None] == 9 * of[None] + 8)) * 1.0
    out["spread_sum4"] = ((p[:, None] // 32 == p[None] // 32) & (nine[:, None] == 8)) * 1.0
    out["minus_ident"] = -np.eye(128)
    out["own_chunk"] = (p[:, None] - 96 == np.arange(8)[None]) * 1.0
    at, parts = {}, []
    n = 0
    for k, a in out.items():
        at[k] = (n, a.shape[1])
        parts.append(a.astype(np.float32))
        n += a.shape[1]
    return np.concatenate(parts, axis=1), at


def spread(ap, axis, n):
    ap = ap.unsqueeze(axis)
    shape = list(ap.shape)
    shape[axis] = n
    return ap.broadcast_to(shape)


def chunk(t, c):
    return t[:, c * CW:(c + 1) * CW]


class Flow:

    CREDIT = 2

    def __init__(self, sem, per=1):
        self.sem, self.per = sem, per

    def inc(self, instruction):
        instruction.then_inc(self.sem, 1)

    def wait(self, engine, slot, k=None):
        k = self.per if k is None else k
        engine.wait_ge(self.sem, slot * self.per + (self.CREDIT * self.per + k))


def give(engine, *flows):
    for f in flows:
        engine.sem_inc(f.sem, f.CREDIT * f.per)


def rolled(engine, n, slot, lag=None, slot2=None):
    slot(0, 0, 0)
    if slot2:
        slot2(0, 0, 0)

    def both(p, u, h):
        slot(p, u, h)
        if lag:
            lag(p - 1, 1 - u, h - 1 + u)
        if slot2:
            slot2(p, u, h)

    with engine.Fori(0, (n - 1) // 2) as turn:
        for v in (1, 2):
            both(turn * 2 + v, v % 2, turn + v // 2)
    if n % 2 == 0:
        both(n - 1, 1, n // 2 - 1)
    if lag:
        lag(n - 1, (n - 1) % 2, (n - 1) // 2)


def by_four(engine, slot):
    for w in range(4):
        slot(w, w, 0)
    with engine.Fori(0, PAIRS // 4 - 1) as turn:
        for w in range(4):
            slot(turn * 4 + (w + 4), w, turn + 1)


def head_mask4(c_, k):
    return spread(spread(c_["head_in_group"], 2, L), 1, k)


class Shared:

    def semaphore(self, name):
        self.semaphores.append(self.nc.alloc_semaphore(name=name))
        return self.semaphores[-1]


def normalize(g, tag):
    nc = g.nc
    with ExitStack() as ctx:
        sem = lambda n: g.semaphore(f"{tag}_{n}")
        sq = ctx.enter_context(nc.sbuf_tensor(f"{tag}_sq", [128, NT], F32))
        sd = ctx.enter_context(nc.sbuf_tensor(f"{tag}_sd", [128, NT], F32))
        mean_done, centred, squared, var_done, logged, rooted, normed = (
            sem(n) for n in ("mean", "centred", "squared", "var", "logged", "rooted", "normed"))
        block = ctx.enter_context(nc.Block())

        @block.tensor
        def _(pe):
            for c in range(CH):
                nc.tensor.matmul(g.bank(c)[:, 0:CW], g.c["mean"], chunk(g.xt, c), start=True, stop=True).then_inc(mean_done, 1)
            for c in range(CH):
                pe.wait_ge(squared, c + 1)
                nc.tensor.matmul(g.bank(4 + c)[:, 0:CW], g.c["mean"], chunk(sq, c), start=True, stop=True).then_inc(var_done, 1)

        @block.scalar
        def _(act):
            for c in range(CH):
                act.wait_ge(centred, c + 1)
                nc.scalar.activation(chunk(sq, c), chunk(g.xn, c), ACT.Square).then_inc(squared, 1)
            for c in range(CH):
                act.wait_ge(var_done, c + 1)
                nc.scalar.activation(chunk(sd, c), g.bank(4 + c)[:, 0:CW], ACT.Ln, bias=g.eps_ln[:, 0:1]).then_inc(logged, 1)
                act.wait_ge(logged, c + 1)
                nc.scalar.activation(chunk(sd, c), chunk(sd, c), ACT.Exp, scale=-0.5).then_inc(rooted, 1)

        @block.vector
        def _(dve):
            for c in range(CH):
                dve.wait_ge(mean_done, c + 1)
                nc.vector.tensor_tensor(chunk(g.xn, c), chunk(g.xt, c), g.bank(c)[:, 0:CW], ALU.subtract).then_inc(centred, 1)
            for c in range(CH):
                dve.wait_ge(rooted, c + 1)
                nc.vector.tensor_tensor(chunk(g.xn, c), chunk(g.xn, c), chunk(sd, c), ALU.mult).then_inc(normed, 1)
            dve.wait_ge(normed, CH)


def setup(g):
    nc = g.nc
    with ExitStack() as ctx:
        loaded, filled = (g.semaphore(n) for n in ("loaded", "filled"))
        block = ctx.enter_context(nc.Block())

        @block.sync
        def _(sp):
            sp.dma_start(g.xt[:], g.d["xT"]).then_inc(loaded, 16)
            sp.dma_start(g.consts[:], g.d["consts"]).then_inc(loaded, 16)
            for name in g.small:
                sp.dma_start(g.w[name][:], g.d[name]).then_inc(loaded, 16)
            sp.wait_ge(loaded, 16 * (2 + len(g.small)))

        @block.vector
        def _(dve):
            dve.wait_ge(loaded, 16 * (2 + len(g.small)))
            for name in ("q", "k"):
                plain, turned = (g.w[f"Rw{name}{t}"][:].rearrange("p (a two) -> p a two", two=2) for t in "TS")
                nc.vector.tensor_scalar(turned[:, :, 0], plain[:, :, 1], -1.0, None, ALU.mult).then_inc(filled, 1)
                nc.vector.tensor_copy(turned[:, :, 1], plain[:, :, 0]).then_inc(filled, 1)
            nc.vector.memset(g.eps_ln[:], EPS_LN).then_inc(filled, 1)
            nc.vector.memset(g.eps_rms[:], 1e-6).then_inc(filled, 1)
            nc.vector.memset(g.eps_alpha[:], 1e-8).then_inc(filled, 1)
            nc.vector.memset(g.ps[:], 0.0).then_inc(filled, 1)
            dve.wait_ge(filled, 8)


def retention(g):
    nc, c_ = g.nc, g.c
    with ExitStack() as ctx:
        sem = lambda n: g.semaphore(f"ret_{n}")
        sb = lambda n, s, t=F32: ctx.enter_context(nc.sbuf_tensor(f"ret_{n}", s, t))
        qt = sb("qt", [128, NT])
        xk = sb("xk", [128, 2, NT])
        ot = sb("ot", [128, NT])
        sq = sb("sq", [128, 2, NT])
        decay = sb("decay", [128, PAIRS, H])
        t0, t1 = sb("t0", [128, PAIRS, H]), sb("t1", [128, PAIRS, H])
        kt = xk[:, 1, :]

        projected, squared, summed, rooted, scaled, copied = (
            sem(n) for n in ("projected", "squared", "summed", "rooted", "scaled", "copied"))
        a_done, v_step, s_step, sums_begun = sem("a_done"), sem("v_step"), sem("s_step"), sem("sums_begun")
        limited, logged = sem("limited"), sem("logged")
        with nc.Block() as block:
            @block.tensor
            def _(pe):
                for b in range(B):
                    mm = nc.tensor.matmul(g.bank(7)[64 * (b % 2):64 * (b % 2) + L, H * (b // 2):H * (b // 2) + H],
                                          g.xn[:, b * L:(b + 1) * L], g.w["Wa"][:], start=True, stop=True)
                mm.then_inc(a_done, 1)
                def project(c):
                    if c >= 2:
                        pe.wait_ge(scaled, c - 1)
                    bank = 4 * (c % 2)
                    nc.tensor.matmul(g.bank(bank)[:, 0:CW], g.w["Wq"][:], chunk(g.xn, c), start=True, stop=True)
                    nc.tensor.matmul(g.bank(bank + 1)[:, 0:CW], g.w["Wk"][:], chunk(g.xn, c), start=True, stop=True).then_inc(projected, 1)

                project(0)
                project(1)
                for c in range(CH):
                    pe.wait_ge(squared, c + 1)
                    if c >= 1:
                        pe.wait_ge(limited, c)
                    for k in range(2):
                        mm = nc.tensor.matmul(g.bank(2 + k)[:, 0:CW], c_["head_sum"], chunk(sq[:, k, :], c), start=True, stop=True)
                    mm.then_inc(summed, 1)
                    if 1 <= c < CH - 1:
                        project(c + 1)

            @block.gpsimd
            def _(pool):
                nc.gpsimd.tensor_copy(xk[:, 0, :], g.xn[:]).then_inc(copied, 1)
                pool.wait_ge(copied, 1)

            @block.scalar
            def _(act):
                act.wait_ge(v_step, 1)
                nc.scalar.activation(t1[:], t0[:], ACT.Abs).then_inc(s_step, 1)
                act.wait_ge(s_step, 1)
                nc.scalar.activation(t1[:], t1[:], ACT.Exp, scale=-1.0).then_inc(s_step, 1)
                act.wait_ge(s_step, 2)
                nc.scalar.activation(t1[:], t1[:], ACT.Ln, bias=1.0).then_inc(s_step, 1)
                nc.scalar.activation(g.w["A_log"][:], g.w["A_log"][:], ACT.Exp).then_inc(s_step, 1)
                act.wait_ge(v_step, 3)
                nc.scalar.activation(t1[:], t0[:], ACT.Exp, scale=-1.0).then_inc(s_step, 1)
                act.wait_ge(s_step, 5)
                nc.scalar.activation(decay[:], t1[:], ACT.Ln, bias=g.eps_alpha[:, 0:1]).then_inc(s_step, 1)
                def square(c):
                    act.wait_ge(projected, c + 1)
                    bank = 4 * (c % 2)
                    nc.scalar.activation(sq[:, :, c * CW:(c + 1) * CW], g.ps[:, bank:bank + 2, 0:CW], ACT.Square).then_inc(squared, 1)

                square(0)
                for c in range(CH):
                    if c + 1 < CH:
                        square(c + 1)
                    r = sq[:, :, c * CW:(c + 1) * CW]
                    act.wait_ge(limited, c + 1)
                    nc.scalar.activation(r, r, ACT.Ln).then_inc(logged, 1)
                    act.wait_ge(logged, c + 1)
                    nc.scalar.activation(r, r, ACT.Exp, scale=-0.5).then_inc(rooted, 1)
                act.wait_ge(s_step, 6)

            @block.vector
            def _(dve):
                dve.wait_ge(a_done, 1)
                z_in = g.bank(7)[:, 0:PAIRS * H].rearrange("p (a h) -> p a h", h=H)
                nc.vector.tensor_tensor(t0[:], z_in, spread(g.w["dt_bias"][:], 1, PAIRS), ALU.add).then_inc(v_step, 1)
                dve.wait_ge(s_step, 4)
                nc.vector.scalar_tensor_tensor(out=t0[:], in0=t0[:], scalar=0.0, in1=t1[:], op0=ALU.max, op1=ALU.add).then_inc(v_step, 1)
                dve.wait_ge(v_step, 2)
                nc.vector.tensor_tensor(t0[:], t0[:], spread(g.w["A_log"][:], 1, PAIRS), ALU.mult).then_inc(v_step, 1)
                def limit(c):
                    dve.wait_ge(summed, c + 1)
                    nc.vector.tensor_scalar(sq[:, :, c * CW:(c + 1) * CW], g.ps[:, 2:4, 0:CW], 1e-24, None, ALU.max).then_inc(limited, 1)

                limit(0)
                for c in range(CH):
                    if c + 1 < CH:
                        limit(c + 1)
                    bank = 4 * (c % 2)
                    dve.wait_ge(rooted, c + 1)
                    nc.vector.tensor_tensor(chunk(qt, c), g.bank(bank)[:, 0:CW], chunk(sq[:, 0, :], c), ALU.mult)
                    nc.vector.tensor_tensor(chunk(kt, c), g.bank(bank + 1)[:, 0:CW], chunk(sq[:, 1, :], c), ALU.mult).then_inc(scaled, 1)
                dve.wait_ge(scaled, CH)

        part = [sb(f"part{u}", [128, 2, 2 * L]) for u in range(2)]
        qb = [sb(f"qb{u}", [128, 2, H, L]) for u in range(2)]
        dm = [sb(f"dm{u}", [128, H, L]) for u in range(2)]
        vs = [sb(f"vs{u}", [128, D]) for u in range(2)]
        ee = [sb(f"ee{u}", [128, H, L]) for u in range(2)]
        pp = [sb(f"pp{u}", [128, H, L]) for u in range(2)]
        om = sb("om", [128, 2, HG, L])
        flow = lambda n, per=1: Flow(sem(n), per)
        parted, spreadq, dmade, v_out, v_copied, d_out, exped, masked, scored, weighed, pved, own, reduced = (
            flow(n) for n in ("parted", "spreadq", "dmade", "v_out", "v_copied", "d_out", "exped", "masked", "scored",
                              "weighed", "pved", "own", "reduced"))
        with nc.Block() as block:
            @block.gpsimd
            def _(pool):
                give(pool, spreadq, parted)

                def slot(p, u, h, scores, sums, outputs):
                    if scores:
                        scored.wait(pool, p - 2)
                        for k in range(2):
                            q = qt[:, bass.ds(p * (2 * L) + k * L, L)]
                            t = nc.gpsimd.tensor_tensor(qb[u][:, k], spread(q, 1, H), spread(c_["head_of"], 2, L), ALU.mult)
                        spreadq.inc(t)
                        parted.inc(nc.gpsimd.tensor_copy(part[u][:], xk[:, :, bass.ds(p * (2 * L), 2 * L)]))

                staged(pool, PAIRS, slot)

            @block.tensor
            def _(pe):
                give(pe, v_out, d_out, scored, pved)

                def slot(p, u, h, scores, sums, outputs):
                    if scores:
                        parted.wait(pe, p)
                        v_copied.wait(pe, p - 1)
                        for k in range(2):
                            mm = nc.tensor.matmul(g.bank(0)[64 * k:64 * k + L, 0:D], part[u][:, 0, k * L:k * L + L], g.w["Wv"][:], start=True, stop=True)
                        v_out.inc(mm)
                        dmade.wait(pe, p)
                        exped.wait(pe, p - 1)
                        for k in range(2):
                            mm = nc.tensor.matmul(g.ps[:, 2 + k, 0:CW], c_["after"], dm[u][:, 8 * k:8 * k + 8, :], start=True, stop=True)
                        d_out.inc(mm)
                        spreadq.wait(pe, p)
                        weighed.wait(pe, p - 1)
                        for n in range(2):
                            for k in range(2):
                                mm = nc.tensor.matmul(g.ps[64 * k:64 * k + L, 4 + n, 0:CW], part[u][:, 1, k * L:k * L + L],
                                                      qb[u][:, k, 8 * n:8 * n + 8, :], start=True, stop=True)
                        scored.inc(mm)
                    if sums:
                        weighed.wait(pe, p - 1)
                        v_copied.wait(pe, p - 1)
                        own.wait(pe, p - 2)
                        pe.sem_inc(sums_begun, 1)
                        for k in range(2):
                            for j in range(G):
                                mm = nc.tensor.matmul(g.ps[32 * j:32 * j + 32, 6 + k, 0:HG * L],
                                                      vs[1 - u][64 * k:64 * k + L, 32 * j:32 * j + 32],
                                                      pp[1 - u][64 * k:64 * k + L, HG * j:HG * j + HG, :], start=True, stop=True)
                        pved.inc(mm)

                staged(pe, PAIRS, slot)

            @block.scalar
            def _(act):
                give(act, v_copied, exped)

                def slot(p, u, h, scores, sums, outputs):
                    if scores:
                        v_out.wait(act, p)
                        pved.wait(act, p - 2)
                        v_copied.inc(nc.scalar.copy(vs[u][:], g.bank(0)[:, 0:D]))
                        d_out.wait(act, p)
                        weighed.wait(act, p - 2)
                        exped.inc(nc.scalar.activation(ee[u][:].rearrange("p (n h) i -> p n (h i)", n=2), g.ps[:, 2:4, 0:CW], ACT.Exp))

                staged(act, PAIRS, slot)

            @block.vector
            def _(dve):
                give(dve, dmade, masked, weighed, own, reduced)

                def slot(p, u, h, scores, sums, outputs):
                    if scores:
                        d_out.wait(dve, p - 2)
                        a = decay[:].rearrange("p a h -> p (a h)")[:, bass.ds(p * H, H)]
                        dmade.inc(nc.vector.tensor_tensor(dm[u][:], spread(a, 2, L), spread(c_["upto"], 1, H), ALU.mult))
                    if sums:
                        q, e = p - 1, ee[1 - u]
                        exped.wait(dve, q)
                        masked.inc(nc.vector.tensor_tensor(e[:], e[:], spread(c_["upto"], 1, H), ALU.mult))
                        masked.wait(dve, q)
                        scored.wait(dve, q)
                        pved.wait(dve, q - 2)
                        weighed.inc(nc.vector.tensor_tensor(pp[1 - u][:].rearrange("p (n h) i -> p n (h i)", n=2), g.ps[:, 4:6, 0:CW],
                                                            e[:].rearrange("p (n h) i -> p n (h i)", n=2), ALU.mult))
                    if outputs:
                        q = p - 2
                        pved.wait(dve, q)
                        reduced.wait(dve, q - 1)
                        own.inc(nc.vector.tensor_tensor(om[:], g.ps[:, 6:8, 0:HG * L].rearrange("p k (h i) -> p k h i", h=HG),
                                                        head_mask4(c_, 2), ALU.mult))
                        own.wait(dve, q)
                        reduced.inc(nc.vector.tensor_reduce(ot[:, bass.ds(q * (2 * L), 2 * L)].rearrange("p (k i) -> p k i", k=2),
                                                            om[:].rearrange("p k h i -> p k i h"), AX_X, ALU.add))

                staged(dve, PAIRS, slot)
                reduced.wait(dve, PAIRS - 1)

        sq1, sq2, gt = sq[:, 0, :], sq[:, 1, :], qt
        squared2, meaned, rooted2, logged2, normed2, gate_out, gated, gmul, projected2, added, wmul = (
            sem(n) for n in ("squared2", "meaned", "rooted2", "logged2", "normed2", "gate_out", "gated", "gmul", "projected2", "added", "wmul"))
        with nc.Block() as block:
            @block.tensor
            def _(pe):
                for c in range(CH):
                    nc.tensor.matmul(g.bank(c)[:, 0:CW], g.w["Wg"][:], chunk(g.xn, c), start=True, stop=True).then_inc(gate_out, 1)
                for c in range(CH):
                    pe.wait_ge(squared2, c + 1)
                    nc.tensor.matmul(g.bank(4 + c)[:, 0:CW], c_["head_mean"], chunk(sq1, c), start=True, stop=True).then_inc(meaned, 1)
                for c in range(CH):
                    pe.wait_ge(gmul, c + 1)
                    nc.tensor.matmul(g.bank(c)[:, 0:CW], g.w["Wo"][:], chunk(ot, c), start=True, stop=True).then_inc(projected2, 1)

            @block.scalar
            def _(act):
                for c in range(CH):
                    nc.scalar.activation(chunk(sq1, c), chunk(ot, c), ACT.Square).then_inc(squared2, 1)
                for c in range(CH):
                    act.wait_ge(gate_out, c + 1)
                    nc.scalar.activation(chunk(gt, c), g.bank(c)[:, 0:CW], ACT.Silu).then_inc(gated, 1)
                for c in range(CH):
                    act.wait_ge(meaned, c + 1)
                    nc.scalar.activation(chunk(sq2, c), g.bank(4 + c)[:, 0:CW], ACT.Ln, bias=g.eps_rms[:, 0:1]).then_inc(logged2, 1)
                    act.wait_ge(logged2, c + 1)
                    nc.scalar.activation(chunk(sq2, c), chunk(sq2, c), ACT.Exp, scale=-0.5).then_inc(rooted2, 1)

            @block.vector
            def _(dve):
                for c in range(CH):
                    dve.wait_ge(rooted2, c + 1)
                    nc.vector.tensor_tensor(chunk(ot, c), chunk(ot, c), chunk(sq2, c), ALU.mult).then_inc(normed2, 1)
                    dve.wait_ge(normed2, c + 1)
                    dve.wait_ge(gated, c + 1)
                    nc.vector.scalar_tensor_tensor(out=chunk(ot, c), in0=chunk(ot, c), scalar=g.w["rms_w"][:, 0:1], in1=chunk(gt, c),
                                                   op0=ALU.mult, op1=ALU.mult).then_inc(gmul, 1)
                for c in range(CH):
                    dve.wait_ge(projected2, c + 1)
                    nc.vector.tensor_tensor(chunk(g.xt, c), chunk(g.xt, c), g.bank(c)[:, 0:CW], ALU.add).then_inc(added, 1)
                dve.wait_ge(added, CH)


def project_back(g, tag, weight, source, bias=None):
    nc = g.nc
    with ExitStack() as ctx:
        projected, added = (g.semaphore(f"{tag}_{n}") for n in ("projected", "added"))
        block = ctx.enter_context(nc.Block())

        @block.tensor
        def _(pe):
            for c in range(CH):
                nc.tensor.matmul(g.bank(c)[:, 0:CW], weight, chunk(source, c), start=True, stop=True).then_inc(projected, 1)

        @block.vector
        def _(dve):
            for c in range(CH):
                dve.wait_ge(projected, c + 1)
                x = chunk(g.xt, c)
                if bias is None:
                    t = nc.vector.tensor_tensor(x, x, g.bank(c)[:, 0:CW], ALU.add)
                else:
                    t = nc.vector.scalar_tensor_tensor(out=x, in0=g.bank(c)[:, 0:CW], scalar=bias, in1=x, op0=ALU.add, op1=ALU.add)
                t.then_inc(added, 1)
            dve.wait_ge(added, CH)


def context_attention(g):
    nc, c_ = g.nc, g.c
    scale = 1.0 / float(np.float32(D) ** 0.5)
    with ExitStack() as ctx:
        sem = lambda n: g.semaphore(f"ctx_{n}")
        flow = lambda n, per=1: Flow(sem(n), per)
        sb = lambda n, s, t=F32: ctx.enter_context(nc.sbuf_tensor(f"ctx_{n}", s, t))
        qq = sb("qq", [128, 2, NT])
        zt = sb("zt", [128, NT])
        q_out, q_done, k_out, k_done = sem("q_out"), sem("q_done"), sem("k_out"), sem("k_done")
        with nc.Block() as block:
            @block.tensor
            def _(pe):
                for c in range(CH):
                    nc.tensor.matmul(g.bank(c)[:, 0:CW], g.w["XWq"][:], chunk(g.xn, c), start=True, stop=True).then_inc(q_out, 1)
                for c in range(CH):
                    pe.wait_ge(q_done, c + 1)
                    nc.tensor.matmul(g.bank(4 + c)[:, 0:CW], g.w["XWkT"][:], chunk(qq[:, 0, :], c), start=True, stop=True).then_inc(k_out, 1)

            @block.vector
            def _(dve):
                for c in range(CH):
                    dve.wait_ge(q_out, c + 1)
                    nc.vector.tensor_scalar(chunk(qq[:, 0, :], c), g.bank(c)[:, 0:CW], g.w["Xbq"][:, 0:1], None, ALU.add).then_inc(q_done, 1)
                dve.wait_ge(q_done, CH)

            @block.scalar
            def _(act):
                for c in range(CH):
                    act.wait_ge(k_out, c + 1)
                    nc.scalar.copy(chunk(qq[:, 1, :], c), g.bank(4 + c)[:, 0:CW]).then_inc(k_done, 1)
                act.wait_ge(k_done, CH)

        cx = [[sb(f"cx{w}{k}", [SW, ST, D]) for k in range(2)] for w in range(4)]
        ct = [sb(f"ct{k}", [128, 3, SB]) for k in range(2)]
        part = [sb(f"part{u}", [128, 2, 2 * L]) for u in range(2)]
        pr = [sb(f"pr{u}", [128, 3 * SB]) for u in range(2)]
        pt = sb("pt", [SW, ST, 128])
        z = sb("z", [128, 128])
        small = sb("small", [128, 2, 5])
        loaded = [sem(f"loaded{w}") for w in range(4)]
        parted, turned, c_copied, scored, peaked, exped, inverted, p_turned, p_copied, pved, divided, z_turned, z_copied = (
            flow(n, k) for n, k in (("parted", 1), ("turned", 6), ("c_copied", 6), ("scored", 1), ("peaked", 3), ("exped", 1),
                                    ("inverted", 1), ("p_turned", 3), ("p_copied", 3), ("pved", 1), ("divided", 1), ("z_turned", 1), ("z_copied", 1)))
        SUMS, TURN = slice(0, 128), slice(128, 256)

        with nc.Block() as block:
            @block.sync
            def _(sp):
                def slot(p, w, f):
                    if not isinstance(p, int) or p >= 4:
                        pved.wait(sp, p - 4)
                    for k in range(2):
                        for a, b in ((0, 112), (112, SW)):
                            src = g.d["ctx"][p * 2 + k].rearrange("(p t) d -> p t d", t=ST)
                            sp.dma_start(cx[w][k][a:b], src[a:b]).then_inc(loaded[w], 16)

                by_four(sp, slot)

            @block.tensor
            def _(pe):
                give(pe, turned, scored, p_turned, pved, z_turned)

                def turn_sums(p):
                    divided.wait(pe, p)
                    z_turned.inc(nc.tensor.transpose(g.bank(7)[:, TURN], z[:], c_["ident"]))

                def turn_weights(p, u):
                    exped.wait(pe, p)
                    for n in range(3):
                        p_copied.wait(pe, *((p, n - 1) if n >= 2 else (p - 1, 2 + n)))
                        for t in range(4):
                            mm = nc.tensor.transpose(g.bank(2 + (u + n) % 2)[0:SW, t * 128:t * 128 + 128],
                                                     pr[u][:, (4 * n + t) * SW:(4 * n + t + 1) * SW], c_["ident"])
                        p_turned.inc(mm)

                def weigh(p, w):
                    z_copied.wait(pe, p - 1)
                    for n in range(3):
                        p_copied.wait(pe, p, n + 1)
                        for t in range(4 * n, 4 * n + 4):
                            for k in range(2):
                                mm = nc.tensor.matmul(g.bank(7)[64 * k:64 * k + L, SUMS], pt[:, t, 64 * k:64 * k + L], cx[w][k][:, t, :],
                                                      start=(t == 0), stop=(t == ST - 1), skip_group_check=True)
                    pved.inc(mm)

                def slot(p, w, f):
                    u = w % 2
                    first = isinstance(p, int) and p == 0
                    pe.wait_ge(loaded[w], 64 * f + 64)
                    for k in range(2):
                        for n in range(3):
                            j = 3 * k + n
                            c_copied.wait(pe, *((p, j - 1) if j >= 2 else (p - 1, 5 + j)))
                            for t in range(4):
                                mm = nc.tensor.transpose(g.bank(j % 2)[:, t * SW:t * SW + SW], cx[w][k][:, 4 * n + t, :],
                                                         c_["ident"][0:SW, 0:SW])
                            turned.inc(mm)
                            if j == 3 and (not isinstance(p, int) or p >= 2):
                                turn_sums(p - 2)
                    if not first:
                        turn_weights(p - 1, 1 - u)
                    parted.wait(pe, p)
                    c_copied.wait(pe, p)
                    exped.wait(pe, p - 1)
                    for k in range(2):
                        nc.tensor.matmul(g.bank(6)[64 * k:64 * k + L, SB + 4:SB + 5], part[u][:, 0, k * L:k * L + L], g.w["Xbk"][:],
                                         start=True, stop=True)
                    for n in range(3):
                        for k in range(2):
                            mm = nc.tensor.matmul(g.bank(4 + n)[64 * k:64 * k + L, 0:SB], part[u][:, 1, k * L:k * L + L], ct[k][:, n, :],
                                                  start=True, stop=True)
                    scored.inc(mm)
                    if not first:
                        weigh(p - 1, (w - 1) % 4)

                by_four(pe, slot)
                turn_sums(PAIRS - 2)
                turn_weights(PAIRS - 1, 1)
                weigh(PAIRS - 1, 3)
                turn_sums(PAIRS - 1)

            @block.scalar
            def _(act):
                give(act, c_copied, exped)

                def exponentials(p, u):
                    peaked.wait(act, p)
                    p_turned.wait(act, p - 2)
                    inverted.wait(act, p - 2)
                    exped.inc(nc.scalar.activation(pr[u][:].rearrange("p (n s) -> p n s", n=3), g.ps[:, 4:7, 0:SB], ACT.Exp,
                                                   bias=small[:, u, 2:3], scale=scale, accum_out=small[:, u, 3:4]))

                def slot(p, w, f):
                    if not (isinstance(p, int) and p == 0):
                        exponentials(p - 1, (w - 1) % 2)
                    scored.wait(act, p - 1)
                    for j in range(6):
                        turned.wait(act, p, j + 1)
                        c_copied.inc(nc.scalar.copy(ct[j // 3][:, j % 3, :], g.bank(j % 2)[:, 0:SB]))

                by_four(act, slot)
                exponentials(PAIRS - 1, 1)

            @block.vector
            def _(dve):
                v = nc.vector
                give(dve, parted, peaked, inverted, p_copied, divided, z_copied)

                def copy_sums(p):
                    z_turned.wait(dve, p)
                    z_copied.inc(v.tensor_copy(zt[:, bass.ds(p * (2 * L), 2 * L)].rearrange("p (k i) -> p k i", k=2),
                                               g.bank(7)[:, TURN].rearrange("p (k i) -> p k i", k=2)[:, :, 0:L]))

                def copy_weights(p, u):
                    exped.wait(dve, p)
                    divided.wait(dve, p - 2)
                    inverted.inc(v.reciprocal(small[:, u, 4:5], small[:, u, 3:4]))
                    pved.wait(dve, p - 1)
                    for n in range(3):
                        p_turned.wait(dve, p, n + 1)
                        p_copied.inc(v.tensor_copy(pt[:, 4 * n:4 * n + 4, :].rearrange("p t q -> p (t q)"),
                                                   g.bank(2 + (u + n) % 2)[0:SW, :]))

                def divide(p, u):
                    pved.wait(dve, p)
                    inverted.wait(dve, p)
                    z_turned.wait(dve, p - 1)
                    divided.inc(v.tensor_scalar(z[:], g.bank(7)[:, SUMS], small[:, u, 4:5], None, ALU.mult))

                def peaks(p, u):
                    scored.wait(dve, p)
                    exped.wait(dve, p - 2)
                    c = g.bank(6)[:, SB + 4:SB + 5]
                    peaked.inc(v.tensor_reduce(small[:, u, 0:1], g.ps[:, 4:7, 0:SB], mybir.AxisListType.XY, ALU.max))
                    peaked.wait(dve, p, 1)
                    peaked.inc(v.tensor_tensor(small[:, u, 1:2], small[:, u, 0:1], c, ALU.add))
                    peaked.wait(dve, p, 2)
                    peaked.inc(v.tensor_scalar(small[:, u, 2:3], c, small[:, u, 1:2], scale, ALU.subtract, ALU.mult))

                def slot(p, w, f):
                    u = w % 2
                    scored.wait(dve, p - 2)
                    parted.inc(v.tensor_copy(part[u][:], qq[:, :, bass.ds(p * (2 * L), 2 * L)]))
                    if not isinstance(p, int) or p >= 2:
                        divide(p - 2, u)
                        copy_sums(p - 2)
                    if not (isinstance(p, int) and p == 0):
                        copy_weights(p - 1, 1 - u)
                    peaks(p, u)

                by_four(dve, slot)
                divide(PAIRS - 2, 0)
                copy_sums(PAIRS - 2)
                copy_weights(PAIRS - 1, 1)
                divide(PAIRS - 1, 1)
                copy_sums(PAIRS - 1)
                z_copied.wait(dve, PAIRS - 1)
        project_back(g, "ctxo", g.w["XWv"][:], zt[:], g.w["Xbv"][:, 0:1])

def choose(g, tag, router, capacity=None):
    nc, c_ = g.nc, g.c
    with ExitStack() as ctx:
        sem = lambda n: g.semaphore(f"{tag}_{n}")
        sb = lambda n: ctx.enter_context(nc.sbuf_tensor(f"{tag}_{n}", [128, TT, E], F32))
        sc, hot1, hot2, rest, tmp, w1, w2, pos1, pos2, scan = (sb(n) for n in ("sc", "hot1", "hot2", "rest", "tmp", "w1", "w2", "pos1", "pos2", "scan"))
        row = ctx.enter_context(nc.sbuf_tensor(f"{tag}_row", [128, 8, TT], F32))
        logits_out, centred, exped, stepped, counted, ready, weights_out, copied, kept = (
            sem(n) for n in ("logits_out", "centred", "exped", "stepped", "counted", "ready", "weights_out", "copied", "kept"))
        wide = lambda r: spread(row[:, r, :], 2, E)
        rank = spread(c_["rank"], 1, TT)
        tiles = lambda k: g.bank(k)[:, 0:TT * E].rearrange("p (t e) -> p t e", e=E)
        with nc.Block() as block:
            @block.tensor
            def _(pe):
                for t in range(TT):
                    mm = nc.tensor.matmul(g.bank(0)[:, t * E:t * E + E], g.xn[:, t * 128:t * 128 + 128], router, start=True, stop=True)
                mm.then_inc(logits_out, 1)
                if capacity:
                    pe.wait_ge(ready, 1)
                    flat = lambda t: t[:].rearrange("p t e -> p (t e)")
                    for k, (m, hot) in enumerate((("before", hot1), ("ones", hot1), ("before", hot2), ("ones", hot2))):
                        mm = nc.tensor.matmul(g.bank(1 + k)[:, 0:TT * E], c_[m], flat(hot), start=True, stop=True)
                    mm.then_inc(counted, 1)
                pe.wait_ge(ready, 2 if capacity else 1)
                for t in range(TT):
                    mm = nc.tensor.transpose(g.bank(5 + t // 4 if t < 12 else 0)[0:E, (t % 4) * 128:(t % 4) * 128 + 128], w1[:, t, :], c_["ident"])
                mm.then_inc(weights_out, 1)

            @block.scalar
            def _(act):
                act.wait_ge(centred, 1)
                nc.scalar.activation(sc[:], tmp[:], ACT.Exp).then_inc(exped, 1)
                act.wait_ge(weights_out, 1)
                for k in range(4):
                    n = min(4, TT - 4 * k) * 128
                    nc.scalar.copy(g.ct[:, k * 512:k * 512 + n], g.bank(5 + k if k < 3 else 0)[0:E, 0:n]).then_inc(copied, 1)
                act.wait_ge(copied, 4)

            @block.sync
            def _(sp):
                sp.wait_ge(copied, 4)
                sp.dma_start(g.ct_dram, g.ct[:]).then_inc(kept, 16)
                sp.wait_ge(kept, 16)

            @block.vector
            def _(dve):
                count = [0]
                v = nc.vector

                def step(instruction):
                    count[0] += 1
                    instruction.then_inc(stepped, 1)
                    dve.wait_ge(stepped, count[0])

                dve.wait_ge(logits_out, 1)
                step(v.tensor_reduce(row[:, 0, :], tiles(0), AX_X, ALU.max))
                v.tensor_tensor(tmp[:], tiles(0), wide(0), ALU.subtract).then_inc(centred, 1)
                dve.wait_ge(exped, 1)
                step(v.tensor_reduce(row[:, 0, :], sc[:], AX_X, ALU.add))
                step(v.reciprocal(row[:, 1, :], row[:, 0, :]))
                step(v.tensor_tensor(sc[:], sc[:], wide(1), ALU.mult))

                def best(hot, scores, r):
                    step(v.tensor_reduce(row[:, r, :], scores[:], AX_X, ALU.max))
                    step(v.tensor_tensor(tmp[:], scores[:], wide(r), ALU.is_ge))
                    step(v.tensor_tensor(tmp[:], tmp[:], rank, ALU.mult))
                    step(v.tensor_reduce(row[:, 7, :], tmp[:], AX_X, ALU.max))
                    step(v.tensor_tensor(hot[:], tmp[:], wide(7), ALU.is_equal))

                best(hot1, sc, 2)
                step(v.tensor_tensor(tmp[:], sc[:], hot1[:], ALU.mult))
                step(v.tensor_tensor(rest[:], sc[:], tmp[:], ALU.subtract))
                if capacity is None:
                    step(v.tensor_tensor(rest[:], rest[:], hot1[:], ALU.subtract))
                best(hot2, rest, 3)
                if capacity is not None:
                    v.tensor_copy(row[:, 6, :], row[:, 3, :]).then_inc(ready, 1)
                    dve.wait_ge(counted, 1)
                    for k, (pos, hot) in enumerate(((pos1, hot1), (pos2, hot2))):
                        step(v.tensor_copy(scan[:], tiles(2 + 2 * k)))
                        for n in (1, 2, 4, 8):
                            step(v.tensor_copy(tmp[:], scan[:]))
                            step(v.tensor_tensor(scan[:, n:TT, :], tmp[:, n:TT, :], tmp[:, 0:TT - n, :], ALU.add))
                        step(v.tensor_tensor(tmp[:], scan[:], tiles(2 + 2 * k), ALU.subtract))
                        step(v.tensor_tensor(pos[:], tmp[:], tiles(1 + 2 * k), ALU.add))
                        if k == 0:
                            step(v.tensor_scalar(w2[:, 0, :], scan[:, TT - 1, :], float(capacity), None, ALU.min))
                        else:
                            step(v.tensor_tensor(pos[:], pos[:], spread(w2[:, 0, :], 1, TT), ALU.add))
                    for pos, hot in ((pos1, hot1), (pos2, hot2)):
                        step(v.tensor_scalar(pos[:], pos[:], float(capacity), None, ALU.is_lt))
                        step(v.tensor_tensor(hot[:], hot[:], pos[:], ALU.mult))
                step(v.tensor_tensor(w1[:], sc[:], hot1[:], ALU.mult))
                step(v.tensor_tensor(w2[:], sc[:], hot2[:], ALU.mult))
                step(v.tensor_tensor(w1[:], w1[:], w2[:], ALU.add))
                step(v.tensor_reduce(row[:, 4, :], w1[:], AX_X, ALU.add))
                if capacity is None:
                    step(v.tensor_scalar(row[:, 4, :], row[:, 4, :], EPS32, None, ALU.add))
                else:
                    step(v.tensor_scalar(row[:, 4, :], row[:, 4, :], EPS32, None, ALU.max))
                step(v.reciprocal(row[:, 5, :], row[:, 4, :]))
                v.tensor_tensor(w1[:], w1[:], wide(5), ALU.mult).then_inc(ready, 1)


def experts_relu(g):
    nc, c_ = g.nc, g.c
    UN = CH * FT
    with ExitStack() as ctx:
        sem = lambda n: g.semaphore(f"ffn_{n}")
        flow = lambda n, per=1: Flow(sem(n), per)
        sb = lambda n, s, t=F32: ctx.enter_context(nc.sbuf_tensor(f"ffn_{n}", s, t))
        wg, wu, wd = ([sb(f"{n}{u}", [128, F]) for u in range(2)] for n in ("wg", "wu", "wd"))
        cb = [sb(f"cb{u}", [128, NT]) for u in range(2)]
        xg = [sb(f"xg{u}", [128, NT]) for u in range(2)]
        rg, hh = sb("rg", [128, 2, CW]), sb("hh", [128, 2, CW])
        zeros = sb("zeros", [128, 128])
        loaded = [sem(f"loaded{u}") for u in range(2)]
        zeroed, added = sem("zeroed"), sem("added")
        scaled, up_out, rectified, hidden, down_out = (flow(n, k) for n, k in (
            ("scaled", CH), ("up_out", UN), ("rectified", UN), ("hidden", UN), ("down_out", UN)))
        with nc.Block() as block:
            @block.sync
            def _(sp):
                def slot(e, u, h):
                    down_out.wait(sp, e - 2)
                    sp.dma_start(wg[u][:], g.d["FWgT"][e]).then_inc(loaded[u], 16)
                    sp.dma_start(wu[u][:], g.d["FWuT"][e]).then_inc(loaded[u], 16)
                    sp.dma_start(wd[u][:].rearrange("p (f d) -> p f d", d=D), g.d["FWdT"][e].rearrange("(f p) d -> p f d", p=128)).then_inc(loaded[u], 16)
                    sp.dma_start(cb[u][:], spread(g.ct_dram[e], 0, 128)).then_inc(loaded[u], 16)

                rolled(sp, E, slot)

            @block.tensor
            def _(pe):
                give(pe, up_out, down_out)
                pe.wait_ge(zeroed, 1)
                for c in range(CH):
                    nc.tensor.matmul(g.bank(c)[:, 0:CW], zeros[:], chunk(g.xn, c), start=True, stop=True)

                def down(e, u, j):
                    c, f = divmod(j, FT)
                    hidden.wait(pe, e, j + 1)
                    down_out.inc(nc.tensor.matmul(g.bank(c)[:, 0:CW], wd[u][:, f * 128:f * 128 + 128], hh[:, j % 2, :],
                                                  start=False, stop=True, skip_group_check=True))

                def slot(e, u, h):
                    for j in range(UN):
                        c, f = divmod(j, FT)
                        if j == 0:
                            pe.wait_ge(loaded[u], 64 * h + 64)
                        if f == 0:
                            scaled.wait(pe, e, c + 1)
                        hidden.wait(pe, *((e, j - 1) if j >= 2 else (e - 1, UN - 1 + j)))
                        nc.tensor.matmul(g.bank(4 + 2 * (j % 2))[:, 0:CW], wg[u][:, f * 128:f * 128 + 128], chunk(xg[u], c), start=True, stop=True)
                        up_out.inc(nc.tensor.matmul(g.bank(5 + 2 * (j % 2))[:, 0:CW], wu[u][:, f * 128:f * 128 + 128], chunk(g.xn, c),
                                                    start=True, stop=True))
                        if j >= 1:
                            down(e, u, j - 1)
                        elif not isinstance(e, int) or e > 0:
                            down(e - 1, 1 - u, UN - 1)

                rolled(pe, E, slot)
                down(E - 1, 1, UN - 1)

            @block.scalar
            def _(act):
                give(act, rectified)

                def slot(e, u, h):
                    for j in range(UN):
                        up_out.wait(act, e, j + 1)
                        hidden.wait(act, *((e, j - 1) if j >= 2 else (e - 1, UN - 1 + j)))
                        rectified.inc(nc.scalar.activation(rg[:, j % 2, :], g.bank(4 + 2 * (j % 2))[:, 0:CW], ACT.Relu))

                rolled(act, E, slot)

            @block.vector
            def _(dve):
                nc.vector.memset(zeros[:], 0.0).then_inc(zeroed, 1)
                give(dve, scaled, hidden)

                def slot(e, u, h):
                    dve.wait_ge(loaded[u], 64 * h + 64)
                    up_out.wait(dve, e - 2)
                    for c in range(CH):
                        scaled.inc(nc.vector.tensor_tensor(chunk(xg[u], c), chunk(g.xn, c), chunk(cb[u], c), ALU.mult))
                    for j in range(UN):
                        rectified.wait(dve, e, j + 1)
                        down_out.wait(dve, *((e, j - 1) if j >= 2 else (e - 1, UN - 1 + j)))
                        hidden.inc(nc.vector.tensor_tensor(hh[:, j % 2, :], rg[:, j % 2, :], g.bank(5 + 2 * (j % 2))[:, 0:CW], ALU.mult))

                rolled(dve, E, slot)
                down_out.wait(dve, E - 1)
                for c in range(CH):
                    nc.vector.tensor_tensor(chunk(g.xt, c), chunk(g.xt, c), g.bank(c)[:, 0:CW], ALU.add).then_inc(added, 1)
                dve.wait_ge(added, CH)


def experts0(g):
    choose(g, "top0", g.w["FWrT"][:])
    experts_relu(g)


def causal_attention(g):
    nc, c_ = g.nc, g.c
    scale = DH ** -0.5
    with ExitStack() as ctx:
        sem = lambda n: g.semaphore(f"rot_{n}")
        flow = lambda n, per=1: Flow(sem(n), per)
        sb = lambda n, s, t=F32: ctx.enter_context(nc.sbuf_tensor(f"rot_{n}", s, t))
        xq = sb("xq", [128, 2, NT])
        kt, ot = sb("kt", [128, NT]), sb("ot", [128, NT])
        turned = sb("turned", [128, 2, CW])
        qt = xq[:, 1, :]
        q_out, q_read, half, whole, copied = sem("q_out"), sem("q_read"), sem("half"), sem("whole"), sem("copied")
        sums_begun = sem("sums_begun")
        with nc.Block() as block:
            @block.tensor
            def _(pe):
                n = 0
                for c in range(CH):
                    for plain, swapped in (("RwqT", "RwqS"), ("RwkT", "RwkS")):
                        if n >= 2:
                            pe.wait_ge(whole, n - 1)
                        nc.tensor.matmul(g.bank(2 * (n % 2))[:, 0:CW], g.w[plain][:], chunk(g.xn, c), start=True, stop=True)
                        nc.tensor.matmul(g.bank(2 * (n % 2) + 1)[:, 0:CW], g.w[swapped][:], chunk(g.xn, c), start=True, stop=True).then_inc(q_out, 1)
                        n += 1

            @block.scalar
            def _(act):
                nc.scalar.copy(xq[:, 0, :], g.xn[:]).then_inc(copied, 1)
                act.wait_ge(copied, 1)

            @block.vector
            def _(dve):
                n = 0
                for c in range(CH):
                    for to in (qt, kt[:]):
                        dve.wait_ge(q_out, n + 1)
                        wide = lambda a: a.rearrange("p (b i) -> p b i", i=L)
                        by = lambda name: spread(c_[name], 1, CW // L)
                        nc.vector.tensor_tensor(wide(turned[:, 0, :]), wide(g.bank(2 * (n % 2))[:, 0:CW]), by("cos"), ALU.mult)
                        nc.vector.tensor_tensor(wide(turned[:, 1, :]), wide(g.bank(2 * (n % 2) + 1)[:, 0:CW]), by("sin"), ALU.mult).then_inc(half, 1)
                        dve.wait_ge(half, n + 1)
                        nc.vector.tensor_tensor(chunk(to, c), turned[:, 0, :], turned[:, 1, :], ALU.add).then_inc(whole, 1)
                        dve.wait_ge(whole, n + 1)
                        n += 1

        part = [sb(f"part{u}", [128, 2, 2 * L]) for u in range(2)]
        kb = [sb(f"kb{u}", [128, 2, H, L]) for u in range(2)]
        ss = [sb(f"ss{u}", [128, H, L]) for u in range(2)]
        pp = [sb(f"pp{u}", [128, H, 64]) for u in range(2)]
        vs = [sb(f"vs{u}", [128, 2, D]) for u in range(2)]
        pt = sb("pt", [128, H // 2, 128])
        om = sb("om", [128, 2, 2, 2, L])
        st = sb("st", [128, 2, 3, H])
        parted, spreadk, v_out, v_copied, scored, hidden, peaked, centred, exped, summed, divided, p_turned, p_copied, pved, own, reduced = (
            flow(n, k) for n, k in (("parted", 1), ("spreadk", 1), ("v_out", 1), ("v_copied", 1), ("scored", 1), ("hidden", 1), ("peaked", 1),
                                    ("centred", 1), ("exped", 1), ("summed", 2), ("divided", 1), ("p_turned", 1), ("p_copied", 1),
                                    ("pved", 1), ("own", 1), ("reduced", 1)))
        padded = sem("padded")
        with nc.Block() as block:
            @block.gpsimd
            def _(pool):
                give(pool, spreadk, centred)

                def slot(p, u, h, scores, weights, sums):
                    if scores:
                        scored.wait(pool, p - 2)
                        for k in range(2):
                            t = nc.gpsimd.tensor_tensor(kb[u][:, k], spread(kt[:, bass.ds(p * (2 * L) + k * L, L)], 1, H),
                                                        spread(c_["head_of"], 2, L), ALU.mult)
                        spreadk.inc(t)
                    if weights:
                        peaked.wait(pool, p - 1)
                        a = ss[1 - u]
                        centred.inc(nc.gpsimd.tensor_tensor(a[:], a[:], spread(st[:, 1 - u, 0, :], 2, L), ALU.subtract))

                staged(pool, PAIRS, slot)

            @block.tensor
            def _(pe):
                give(pe, v_out, scored, p_turned, pved)

                def slot(p, u, h, scores, weights, sums):
                    if scores:
                        spreadk.wait(pe, p)
                        parted.wait(pe, p)
                        hidden.wait(pe, p - 1)
                        for n in range(2):
                            for k in range(2):
                                mm = nc.tensor.matmul(g.bank(4 + n)[64 * k:64 * k + L, 0:CW], part[u][:, 1, k * L:k * L + L],
                                                      kb[u][:, k, 8 * n:8 * n + 8, :], start=True, stop=True)
                        scored.inc(mm)
                    if sums:
                        q = p - 2
                        divided.wait(pe, q)
                        p_copied.wait(pe, q - 1)
                        for n in range(H // 2):
                            mm = nc.tensor.transpose(g.bank(2 + n // 4)[:, (n % 4) * 128:(n % 4) * 128 + 128],
                                                     pp[u][:, 2 * n:2 * n + 2, :].rearrange("p h j -> p (h j)"), c_["ident"])
                        p_turned.inc(mm)
                    if scores:
                        v_copied.wait(pe, p - 1)
                        for k in range(2):
                            for v in range(2):
                                mm = nc.tensor.matmul(g.bank(0)[64 * v:64 * v + L, k * D:k * D + D], part[u][:, 0, k * L:k * L + L], g.w["RwvT"][:],
                                                      start=True, stop=True)
                        v_out.inc(mm)
                    if sums:
                        q = p - 2
                        p_copied.wait(pe, q)
                        v_copied.wait(pe, q)
                        own.wait(pe, q - 1)
                        pe.sem_inc(sums_begun, 1)
                        for k in range(2):
                            for n in range(H // 2):
                                for v in range(2):
                                    j = n // 2
                                    mm = nc.tensor.matmul(g.bank(6 + v)[32 * j:32 * j + 32, (2 * k + n % 2) * L:(2 * k + n % 2 + 1) * L],
                                                          vs[u][64 * v:64 * v + L, k, 32 * j:32 * j + 32],
                                                          pt[64 * v:64 * v + L, n, 64 * k:64 * k + L], start=True, stop=True)
                        pved.inc(mm)

                staged(pe, PAIRS, slot)

            @block.scalar
            def _(act):
                give(act, parted, v_copied, exped, p_copied)

                def slot(p, u, h, scores, weights, sums):
                    if scores:
                        scored.wait(act, p - 2)
                        v_out.wait(act, p - 2)
                        parted.inc(nc.scalar.copy(part[u][:], xq[:, :, bass.ds(p * (2 * L), 2 * L)]))
                    if weights:
                        q, a = p - 1, ss[1 - u]
                        centred.wait(act, q)
                        exped.inc(nc.scalar.activation(a[:], a[:], ACT.Exp, scale=scale))
                    if sums:
                        q = p - 2
                        p_turned.wait(act, q)
                        pved.wait(act, q - 1)
                        p_copied.inc(nc.scalar.copy(pt[:].rearrange("p (a n) i -> p a (n i)", a=2), g.ps[:, 2:4, :]))
                    if scores:
                        v_out.wait(act, p)
                        pved.wait(act, p - 2)
                        v_copied.inc(nc.scalar.copy(vs[u][:], g.bank(0)[:, 0:2 * D].rearrange("p (k d) -> p k d", k=2)))

                staged(act, PAIRS, slot)

            @block.vector
            def _(dve):
                for u in range(2):
                    nc.vector.memset(pp[u][:], 0.0).then_inc(padded, 1)
                dve.wait_ge(padded, 2)
                give(dve, hidden, peaked, summed, divided, own, reduced)

                def slot(p, u, h, scores, weights, sums):
                    if scores:
                        scored.wait(dve, p)
                        divided.wait(dve, p - 2)
                        hidden.inc(nc.vector.tensor_tensor(ss[u][:].rearrange("p (n h) i -> p n h i", n=2),
                                                           g.ps[:, 4:6, 0:CW].rearrange("p n (h i) -> p n h i", i=L),
                                                           spread(spread(c_["hide"], 1, 8), 1, 2), ALU.add))
                        hidden.wait(dve, p)
                        centred.wait(dve, p - 2)
                        peaked.inc(nc.vector.tensor_reduce(st[:, u, 0, :], ss[u][:], AX_X, ALU.max))
                    if weights:
                        q, a = p - 1, ss[1 - u]
                        exped.wait(dve, q)
                        summed.inc(nc.vector.tensor_reduce(st[:, 1 - u, 1, :], a[:], AX_X, ALU.add))
                        summed.wait(dve, q, 1)
                        summed.inc(nc.vector.reciprocal(st[:, 1 - u, 2, :], st[:, 1 - u, 1, :]))
                        summed.wait(dve, q, 2)
                        p_turned.wait(dve, q - 2)
                        divided.inc(nc.vector.tensor_tensor(pp[1 - u][:, :, 0:L], a[:], spread(st[:, 1 - u, 2, :], 2, L), ALU.mult))
                    if sums:
                        q = p - 2
                        pved.wait(dve, q)
                        reduced.wait(dve, q - 1)
                        mask = c_["head_in_group"].rearrange("p (n v) -> p v n", v=2)
                        for k in range(2):
                            t = nc.vector.tensor_tensor(om[:, k], g.ps[:, 6:8, k * 2 * L:(k + 1) * 2 * L].rearrange("p v (n i) -> p v n i", i=L),
                                                        spread(mask, 3, L), ALU.mult)
                        own.inc(t)
                        own.wait(dve, q)
                        reduced.inc(nc.vector.tensor_reduce(ot[:, bass.ds(q * (2 * L), 2 * L)].rearrange("p (k i) -> p k i", k=2),
                                                            om[:].rearrange("p k v n i -> p k i (v n)"), AX_X, ALU.add))

                staged(dve, PAIRS, slot)
                reduced.wait(dve, PAIRS - 1)
        project_back(g, "roto", g.w["RwoT"][:], ot[:])

def head_attention(g):
    nc, c_ = g.nc, g.c
    scale = DH ** -0.5
    QW = HG * L
    V9 = DH + 1
    PEAKS = 2 * G * 3
    with ExitStack() as ctx:
        sem = lambda n: g.semaphore(f"hat_{n}")
        flow = lambda n, per=1: Flow(sem(n), per)
        sb = lambda n, s, t=F32: ctx.enter_context(nc.sbuf_tensor(f"hat_{n}", s, t))
        ct = [sb(f"ct{u}", [128, S]) for u in range(2)]
        kf, kl = sb("kf", [128, S]), sb("kl", [128, S], F32R)
        kh = [sb(f"kh{u}", [128, S], F32R) for u in range(2)]
        qn = sb("qn", [128, L], F32R)
        qm = [sb(f"qm{u}", [128, HG, L], F32R) for u in range(2)]
        k3 = [sb(f"k3{u}", [128, G, S], F32R) for u in range(2)]
        q3 = [sb(f"q3{u}", [128, G, QW], F32R) for u in range(2)]
        qf, qs = sb("qf", [96, G, L]), sb("qs", [96, G, L], F32R)
        vs = [sb(f"vs{u}", [SW, ST, H, V9]) for u in range(2)]
        pb = [sb(f"pb{k}", [SW, H * L]) for k in range(3)]
        tops, top = sb("tops", [128, 2 * G, 3]), sb("top", [128, 2 * G])
        om, on, rc = sb("om", [128, 3, L]), sb("on", [128, 2, L]), sb("rc", [128, 2, L])
        ot = sb("ot", [128, 2, NT])
        loaded, placed = ([sem(f"{n}{u}") for u in range(2)] for n in ("loaded", "placed"))
        (n_out, n_copied, n_spread, k_full, v_out, v_copied, q_out, q_split, q_spread, peak_out, peaked, topped, top_out, shifted, k_out, k_high, k_low,
         scored, exped, summed, own, picked, sum_out, inverted, normed) = (flow(n, k) for n, k in (
            ("n_out", 1), ("n_copied", 1), ("n_spread", 1), ("k_full", 3),
            ("v_out", 3), ("v_copied", 3), ("q_out", 1), ("q_split", 3), ("q_spread", 1), ("peak_out", PEAKS), ("peaked", PEAKS),
            ("topped", 1), ("top_out", 1), ("shifted", 1), ("k_out", 3), ("k_high", 3), ("k_low", 3),
            ("scored", ST), ("exped", ST), ("summed", ST), ("own", 1), ("picked", 2), ("sum_out", 1), ("inverted", 1), ("normed", 1)))
        projected, filled, added, biased = sem("projected"), sem("filled"), sem("added"), sem("biased")
        MISC, PV, PK, LAST = 7, 6, 4, 5
        NEXT, SUMS = G * L, G * L + L
        V_AT, Q_AT, K_AT = 1, 5, 7
        AT = [2, 3, 3, 3, 2, 1, 2, 3, 3, 2, 0, 0]
        BEFORE = [sum(AT[:t]) for t in range(ST)]
        peak_of = lambda m: (m % G, (m // G) % 2, m // (2 * G))

        with nc.Block() as block:
            @block.sync
            def _(sp):
                def slot(p, u, h, keys, maxima, sums):
                    if keys:
                        v_out.wait(sp, p - 2)
                        k_out.wait(sp, p - 2)
                        sp.dma_start(ct[u][:], g.d["ctxT"][p]).then_inc(loaded[u], 16)
                    if maxima:
                        q = p - 1
                        k_high.wait(sp, q)
                        k_low.wait(sp, q)
                        scored.wait(sp, q - 2)
                        for n, part in enumerate((kh[1 - u], kl, kh[1 - u])):
                            for j in range(G):
                                sp.dma_start(k3[1 - u][32 * n:32 * n + 32, j, :].bitcast(F32), part[32 * j:32 * j + 32, :].bitcast(F32)).then_inc(placed[1 - u], 16)

                staged(sp, B, slot)

            @block.tensor
            def _(pe):
                give(pe, n_out, v_out, q_out, peak_out, top_out, k_out, scored, summed, sum_out)
                pe.wait_ge(filled, 7)

                def sum_weights(q):
                    picked.wait(pe, q)
                    normed.wait(pe, q - 1)
                    nc.tensor.matmul(g.bank(MISC)[:, SUMS:SUMS + L], c_["spread_sum"], on[:, 0, :], start=True, stop=True)
                    sum_out.inc(nc.tensor.matmul(g.bank(MISC)[:, SUMS + L:SUMS + 2 * L], c_["spread_sum4"], on[:, 1, :], start=True, stop=True))

                def peaks(q, u, m0, n):
                    for m in range(m0, m0 + n):
                        peaked.wait(pe, *((q, m - 1) if m >= 2 else (q - 1, PEAKS - 1 + m)))
                        if m == 1:
                            shifted.wait(pe, q - 1)
                        j, r, c = peak_of(m)
                        peak_out.inc(nc.tensor.matmul(g.bank(PK + m % 2)[0:2 * L, 0:SB], qm[1 - u][32 * j:32 * j + 32, 2 * r:2 * r + 2, :],
                                                      kh[1 - u][32 * j:32 * j + 32, c * SB:(c + 1) * SB], start=True, stop=True))

                def weigh(q, u, t):
                    exped.wait(pe, q, t + 1)
                    if t == 0:
                        picked.wait(pe, q - 1)
                        v_copied.wait(pe, q)
                    for n, w in ((0, 3), (3, 1)):
                        for j in range(G):
                            mm = nc.tensor.matmul(g.bank(PV)[32 * j:32 * j + V9 * w, n * L:(n + w) * L],
                                                  vs[u][:, t, HG * j + n:HG * j + n + w, :].rearrange("p h e -> p (h e)"),
                                                  pb[t % 3][:, (HG * j + n) * L:(HG * j + n + w) * L],
                                                  start=(t == 0 and n == 0), stop=(t == ST - 1), skip_group_check=True)
                    summed.inc(mm)

                def slot(p, u, h, keys, maxima, sums):
                    for t in range(ST):
                        if sums:
                            q = p - 2
                            if t == 0:
                                q_spread.wait(pe, q)
                                shifted.wait(pe, q)
                                pe.wait_ge(placed[u], 12 * 16 * h)
                            exped.wait(pe, *((q, t - 1) if t >= 2 else (q - 1, ST - 1 + t)))
                            for j in range(G):
                                mm = nc.tensor.matmul(g.bank(2 * (t % 2) + j // 2)[0:SW, (j % 2) * QW:(j % 2 + 1) * QW],
                                                      k3[u][:, j, t * SW:(t + 1) * SW], q3[u][:, j, :], start=True, stop=True)
                            scored.inc(mm)
                        if maxima:
                            if t == 0:
                                n_spread.wait(pe, p - 1)
                                k_high.wait(pe, p - 1)
                            peaks(p - 1, u, BEFORE[t], min(2, AT[t]))
                        if maxima and 0 <= t - V_AT < 3:
                            n = t - V_AT
                            if n == 0:
                                k_full.wait(pe, p - 1)
                            else:
                                v_copied.wait(pe, p - 1, n)
                            for i in range(4 * n, 4 * n + 4):
                                mm = nc.tensor.matmul(g.bank(MISC)[0:SW, (i % 4) * D:(i % 4 + 1) * D], ct[1 - u][:, i * SW:(i + 1) * SW],
                                                      g.w["HWvT"][:], start=True, stop=True)
                            v_out.inc(mm)
                        if t == Q_AT:
                            if maxima:
                                v_copied.wait(pe, p - 1, 3)
                                for j in range(G):
                                    mm = nc.tensor.matmul(g.bank(MISC)[0:96, j * L:(j + 1) * L], g.w["HWq3"][:, 96 * j:96 * j + 96],
                                                          g.xn[:, bass.ds((p - 1) * L, L)], start=True, stop=True)
                                q_out.inc(mm)
                            if keys:
                                n_out.inc(nc.tensor.matmul(g.bank(MISC)[:, NEXT:NEXT + L], g.w["HWqT"][:], g.xn[:, bass.ds(p * L, L)],
                                                           start=True, stop=True))
                            if sums and (not isinstance(p, int) or p >= 3):
                                sum_weights(p - 3)
                        if keys and 0 <= t - K_AT < 3:
                            n = t - K_AT
                            if n == 0:
                                pe.wait_ge(loaded[u], 16 * h + 16)
                                q_split.wait(pe, p - 1, 1)
                                n_copied.wait(pe, p)
                                normed.wait(pe, p - 3)
                            else:
                                k_full.wait(pe, p, n)
                            k_out.inc(nc.tensor.matmul(g.bank(MISC)[:, 0:SB], g.w["HWkT"][:], ct[u][:, n * SB:(n + 1) * SB], start=True, stop=True))
                        if maxima and t == 10:
                            topped.wait(pe, p - 1)
                            top_out.inc(nc.tensor.matmul(g.bank(LAST)[96:96 + 2 * G, 0:2 * L], top[0:2 * L, :], c_["minus_ident"][0:2 * L, 0:2 * L],
                                                         start=True, stop=True))
                        if maxima:
                            peaks(p - 1, u, BEFORE[t] + min(2, AT[t]), AT[t] - min(2, AT[t]))
                        if t == 0 and sums and (not isinstance(p, int) or p >= 3):
                            weigh(p - 3, 1 - u, ST - 1)
                        if t == 2 and sums:
                            weigh(p - 2, u, 0)
                        if t >= 2 and sums:
                            weigh(p - 2, u, t - 1)

                staged(pe, B, slot)
                weigh(B - 1, 1, ST - 1)
                sum_weights(B - 1)
                pe.wait_ge(biased, CH)
                for c in range(CH):
                    for n in range(2):
                        mm = nc.tensor.matmul(g.bank(c)[:, 0:CW], g.w[f"HWo{n}"][:], chunk(ot[:, n, :], c), start=(n == 0), stop=(n == 1))
                    mm.then_inc(projected, 1)

            @block.scalar
            def _(act):
                give(act, v_copied, k_full, k_high, exped)

                def slot(p, u, h, keys, maxima, sums):
                    for t in range(ST):
                        if sums:
                            q = p - 2
                            scored.wait(act, q, t + 1)
                            summed.wait(act, *((q, t - 2) if t >= 3 else (q - 1, ST - 2 + t)))
                            exped.inc(nc.scalar.activation(pb[t % 3][:].rearrange("p (n i) -> p n i", n=2), g.ps[0:SW, 2 * (t % 2):2 * (t % 2) + 2, 0:2 * QW],
                                                           ACT.Exp, scale=scale))
                        if maxima and 0 <= t - V_AT < 3:
                            n = t - V_AT
                            v_out.wait(act, p - 1, n + 1)
                            if n == 0:
                                summed.wait(act, p - 3)
                            v_copied.inc(nc.scalar.copy(vs[1 - u][:, 4 * n:4 * n + 4, :, 0:DH],
                                                        g.bank(MISC)[0:SW, :].rearrange("p (t h e) -> p t h e", t=4, e=DH)))
                        if maxima and t == Q_AT:
                            q_split.wait(act, p - 1, 1)
                            q_split.inc(nc.scalar.copy(qs[:], qf[:]))
                        if keys and 0 <= t - K_AT < 3:
                            n = t - K_AT
                            if n == 0:
                                peak_out.wait(act, p - 2)
                                if not isinstance(p, int) or p >= 2:
                                    act.wait_ge(placed[u], 12 * 16 * h)
                            k_out.wait(act, p, n + 1)
                            k_high.inc(nc.scalar.activation(kh[u][:, n * SB:(n + 1) * SB], g.bank(MISC)[:, 0:SB], ACT.Identity, bias=g.w["Hbk"][:, 0:1]))
                            k_low.wait(act, p - 1, n + 1)
                            k_full.inc(nc.scalar.activation(kf[:, n * SB:(n + 1) * SB], g.bank(MISC)[:, 0:SB], ACT.Identity, bias=g.w["Hbk"][:, 0:1]))

                staged(act, B, slot)

            @block.gpsimd
            def _(pool):
                give(pool, q_spread, n_spread, k_low)
                pool.wait_ge(filled, 7)

                def slot(p, u, h, keys, maxima, sums):
                    if maxima:
                        q = p - 1
                        q_split.wait(pool, q, 2)
                        k_low.wait(pool, q)
                        q_split.inc(nc.gpsimd.tensor_tensor(qs[64:96], qf[64:96], qs[64:96].bitcast(F32), ALU.subtract))
                        q_split.wait(pool, q)
                        scored.wait(pool, q - 2)
                        for j in range(G):
                            t = nc.gpsimd.tensor_tensor(q3[1 - u][0:96, j, :].rearrange("p (h i) -> p h i", h=HG), spread(qs[:, j, :], 1, HG),
                                                        spread(c_["head_in_group"][0:96], 2, L), ALU.mult)
                        q_spread.inc(t)
                    if keys:
                        n_copied.wait(pool, p)
                        peak_out.wait(pool, p - 2)
                        n_spread.inc(nc.gpsimd.tensor_tensor(qm[u][:], spread(qn[:], 1, HG), spread(c_["head_in_group"], 2, L), ALU.mult))
                        if not isinstance(p, int) or p >= 1:
                            pool.wait_ge(placed[1 - u], 12 * 16 * (h + u))
                        for n in range(3):
                            cols = slice(n * SB, (n + 1) * SB)
                            k_high.wait(pool, p, n + 1)
                            k_full.wait(pool, p, n + 1)
                            k_low.inc(nc.gpsimd.tensor_tensor(kl[:, cols], kf[:, cols], kh[u][:, cols].bitcast(F32), ALU.subtract))

                staged(pool, B, slot)

            @block.vector
            def _(dve):
                v = nc.vector
                v.memset(g.bank(PV), 0.0).then_inc(filled, 1)
                for u in range(2):
                    v.memset(k3[u][96:128].bitcast(F32), 1.0).then_inc(filled, 1)
                    v.memset(q3[u][96:128].bitcast(F32), 0.0).then_inc(filled, 1)
                    v.memset(vs[u][:, :, :, DH:V9], 1.0).then_inc(filled, 1)
                dve.wait_ge(filled, 7)

                def pick(q):
                    summed.wait(dve, q)
                    picked.wait(dve, q - 1)
                    own.inc(v.tensor_tensor(om[:], g.bank(PV)[:, 0:3 * L].rearrange("p (h i) -> p h i", h=3),
                                            spread(c_["head_of_three"], 2, L), ALU.mult))
                    own.wait(dve, q)
                    normed.wait(dve, q - 1)
                    picked.inc(v.tensor_reduce(on[:, 0, :], om[:].rearrange("p h i -> p i h"), AX_X, ALU.add))
                    picked.inc(v.tensor_copy(on[:, 1, :], g.bank(PV)[:, 3 * L:4 * L]))

                def divide(q):
                    sum_out.wait(dve, q)
                    inverted.inc(v.reciprocal(rc[:], g.bank(MISC)[:, SUMS:SUMS + 2 * L].rearrange("p (n i) -> p n i", n=2)))
                    inverted.wait(dve, q)
                    normed.inc(v.tensor_tensor(ot[:, :, bass.ds(q * L, L)], on[:], rc[:], ALU.mult))

                give(dve, n_copied, q_split, peaked, topped, shifted, own, picked, inverted, normed)

                def slot(p, u, h, keys, maxima, sums):
                    def from_queries():
                        older = sums and (not isinstance(p, int) or p >= 3)
                        if maxima:
                            q_out.wait(dve, p - 1)
                        if keys:
                            n_out.wait(dve, p)
                        if older:
                            sum_out.wait(dve, p - 3)
                        if maxima:
                            q = p - 1
                            q_spread.wait(dve, q - 1)
                            q_split.inc(v.tensor_tensor(qf[:], g.bank(MISC)[0:96, 0:G * L].rearrange("p (g i) -> p g i", g=G),
                                                        spread(g.w["Hbq3"][0:96, :], 2, L), ALU.add))
                        if keys:
                            n_spread.wait(dve, p - 1)
                            n_copied.inc(v.tensor_scalar(qn[:], g.bank(MISC)[:, NEXT:NEXT + L], g.w["Hbq"][:, 0:1], None, ALU.add))
                        if older:
                            divide(p - 3)

                    if not maxima:
                        if sums:
                            pick(p - 3)
                        from_queries()
                    for m in range(PEAKS if maxima else 0):
                        if m == 2 and sums and (not isinstance(p, int) or p >= 3):
                            pick(p - 3)
                        if m == BEFORE[Q_AT + 1]:
                            from_queries()
                        q = p - 1
                        peak_out.wait(dve, q, m + 1)
                        if m == 0:
                            topped.wait(dve, q - 1)
                        j, r, n = peak_of(m)
                        peaked.inc(v.tensor_reduce(tops[0:2 * L, 2 * j + r, n:n + 1], g.bank(PK + m % 2)[0:2 * L, 0:SB], AX_X, ALU.max))
                    if maxima:
                        q = p - 1
                        peaked.wait(dve, q)
                        top_out.wait(dve, q - 1)
                        topped.inc(v.tensor_reduce(top[0:2 * L, :], tops[0:2 * L], AX_X, ALU.max))
                    if maxima:
                        q = p - 1
                        top_out.wait(dve, q)
                        scored.wait(dve, q - 2)
                        shifted.inc(v.tensor_tensor(q3[1 - u][96:96 + 2 * G].rearrange("p g (c i) -> p (g c) i", c=2),
                                                    spread(g.bank(LAST)[96:96 + 2 * G, 0:2 * L], 1, 2 * G),
                                                    spread(c_["own_chunk"][96:96 + 2 * G], 2, 2 * L), ALU.mult))
                staged(dve, B, slot)
                pick(B - 1)
                divide(B - 1)
                normed.wait(dve, B - 1)
                for c in range(CH):
                    for n in range(2):
                        t = v.tensor_scalar(chunk(ot[:, n, :], c), chunk(ot[:, n, :], c), g.w["Hbv2"][:, n:n + 1], None, ALU.add)
                    t.then_inc(biased, 1)
                for c in range(CH):
                    dve.wait_ge(projected, c + 1)
                    x = chunk(g.xt, c)
                    v.scalar_tensor_tensor(out=x, in0=g.bank(c)[:, 0:CW], scalar=g.w["Hbo"][:, 0:1], in1=x, op0=ALU.add, op1=ALU.add).then_inc(added, 1)
                dve.wait_ge(added, CH)


def staged(engine, n, slot):
    slot(0, 0, 0, True, False, False)
    slot(1, 1, 0, True, True, False)
    slot(2, 0, 1, True, True, True)
    slot(3, 1, 1, True, True, True)
    with engine.Fori(0, (n - 4) // 2) as turn:
        slot(turn * 2 + 4, 0, turn + 2, True, True, True)
        slot(turn * 2 + 5, 1, turn + 2, True, True, True)
    slot(n, 0, n // 2, False, True, True)
    slot(n + 1, 1, n // 2, False, False, True)


def experts_silu(g):
    nc, c_ = g.nc, g.c
    UN = CH * FT
    N = E + 1
    with ExitStack() as ctx:
        sem = lambda n: g.semaphore(f"moe_{n}")
        flow = lambda n, per=1: Flow(sem(n), per)
        sb = lambda n, s, t=F32: ctx.enter_context(nc.sbuf_tensor(f"moe_{n}", s, t))
        w1, w2 = ([sb(f"{n}{u}", [128, F]) for u in range(2)] for n in ("w1", "w2"))
        b1 = [sb(f"b1{u}", [128, FT]) for u in range(2)]
        cb = [sb(f"cb{u}", [128, NT]) for u in range(2)]
        ss, hh = sb("ss", [128, 4, CW]), sb("hh", [128, 2, CW])
        cts, tenth = sb("cts", [N, NT]), sb("tenth", [1, NT])
        loaded = [sem(f"loaded{u}") for u in range(2)]
        tenthed, kept, weights_in, added = sem("tenthed"), sem("kept"), sem("weights_in"), sem("added")
        up_out, rectified, hidden, down_out = (flow(n, UN) for n in ("up_out", "rectified", "hidden", "down_out"))
        with nc.Block() as block:
            @block.sync
            def _(sp):
                sp.wait_ge(tenthed, 1)
                sp.dma_start(g.ct9_dram[E:N], tenth[:]).then_inc(kept, 16)
                sp.dma_start(g.ct9_dram[0:E], g.ct[:]).then_inc(kept, 16)
                sp.wait_ge(kept, 32)
                sp.dma_start(cts[:], g.ct9_dram).then_inc(weights_in, 16)

                def slot(e, u, h):
                    down_out.wait(sp, e - 2)
                    sp.dma_start(w1[u][:], g.d["Mw1"][e]).then_inc(loaded[u], 16)
                    sp.dma_start(w2[u][:].rearrange("p (f d) -> p f d", d=D), g.d["Mw2"][e].rearrange("(f p) d -> p f d", p=128)).then_inc(loaded[u], 16)
                    sp.dma_start(b1[u][:], g.d["Mb1"][e]).then_inc(loaded[u], 16)
                    sp.dma_start(cb[u][:], spread(g.ct9_dram[e], 0, 128)).then_inc(loaded[u], 16)

                rolled(sp, N, slot)

            @block.tensor
            def _(pe):
                give(pe, up_out, down_out)
                pe.wait_ge(weights_in, 16)
                for c in range(CH):
                    nc.tensor.matmul(g.bank(c)[:, 0:CW], g.w["Mb2"][:], chunk(cts, c), start=True, stop=True)

                def down(e, u, j):
                    c, f = divmod(j, FT)
                    hidden.wait(pe, e, j + 1)
                    down_out.inc(nc.tensor.matmul(g.bank(c)[:, 0:CW], w2[u][:, f * 128:f * 128 + 128], hh[:, j % 2, :],
                                                  start=False, stop=True, skip_group_check=True))

                def slot(e, u, h):
                    for j in range(UN):
                        c, f = divmod(j, FT)
                        if j == 0:
                            pe.wait_ge(loaded[u], 64 * h + 64)
                        rectified.wait(pe, *((e, j - 3) if j >= 4 else (e - 1, UN - 3 + j)))
                        up_out.inc(nc.tensor.matmul(g.bank(4 + j % 4)[:, 0:CW], w1[u][:, f * 128:f * 128 + 128], chunk(g.xn, c), start=True, stop=True))
                        if j >= 2:
                            down(e, u, j - 2)
                        elif not isinstance(e, int) or e > 0:
                            down(e - 1, 1 - u, UN - 2 + j)

                rolled(pe, N, slot)
                for j in (UN - 2, UN - 1):
                    down(N - 1, (N - 1) % 2, j)

            @block.scalar
            def _(act):
                give(act, rectified)

                def slot(e, u, h):
                    act.wait_ge(loaded[u], 64 * h + 64)
                    for j in range(UN):
                        up_out.wait(act, e, j + 1)
                        hidden.wait(act, *((e, j - 3) if j >= 4 else (e - 1, UN - 3 + j)))
                        rectified.inc(nc.scalar.activation(ss[:, j % 4, :], g.bank(4 + j % 4)[:, 0:CW], ACT.Silu, bias=b1[u][:, j % FT:j % FT + 1]))

                rolled(act, N, slot)

            @block.vector
            def _(dve):
                nc.vector.memset(tenth[:], 0.1).then_inc(tenthed, 1)
                give(dve, hidden)

                def slot(e, u, h):
                    dve.wait_ge(loaded[u], 64 * h + 64)
                    for j in range(UN):
                        rectified.wait(dve, e, j + 1)
                        down_out.wait(dve, *((e, j - 1) if j >= 2 else (e - 1, UN - 1 + j)))
                        hidden.inc(nc.vector.tensor_tensor(hh[:, j % 2, :], ss[:, j % 4, :], chunk(cb[u], j // FT), ALU.mult))

                rolled(dve, N, slot)
                down_out.wait(dve, N - 1)
                for c in range(CH):
                    nc.vector.tensor_tensor(chunk(g.xt, c), chunk(g.xt, c), g.bank(c)[:, 0:CW], ALU.add).then_inc(added, 1)
                dve.wait_ge(added, CH)


def experts1(g):
    choose(g, "top1", g.w["Rrouter"][:], CAPACITY)
    experts_silu(g)


def padded_heads(a):
    out = np.zeros((2, G, 32, a.shape[1]), a.dtype)
    by_head = a.reshape(G, HG, DH, a.shape[1])
    for i in range(3):
        out[0, :, 9 * i:9 * i + DH] = by_head[:, i]
    out[1, :, 0:DH] = by_head[:, 3]
    return out.reshape(2, 128, a.shape[1])


SMALL = {
    "Wq": ("L0_attn_Wq", lambda a: a), "Wk": ("L0_attn_Wk", lambda a: a), "Wv": ("L0_attn_Wv", lambda a: a),
    "Wa": ("L0_attn_Wa", lambda a: a), "Wg": ("L0_attn_Wg", lambda a: a), "Wo": ("L0_attn_Wo", lambda a: a),
    "A_log": ("L0_attn_A_log", lambda a: np.tile(a, (128, 1))), "dt_bias": ("L0_attn_dt_bias", lambda a: np.tile(a, (128, 1))),
    "FWrT": ("L0_ffn_Wr", lambda a: a.T), "Rrouter": ("L1_ffn_router_w", lambda a: a),
    "RwqT": ("L1_attn_wq", lambda a: a.T), "RwqS": ("L1_attn_wq", lambda a: a.T),
    "RwkT": ("L1_attn_wk", lambda a: a.T), "RwkS": ("L1_attn_wk", lambda a: a.T),
    "RwvT": ("L1_attn_wv", lambda a: a.T), "RwoT": ("L1_attn_wo", lambda a: a.T),
    "HWq3": ("L1_xattn_Wq", lambda a: np.repeat(a.T.reshape(D, G, 1, 32), 3, axis=2).reshape(D, G * 96)),
    "Hbq3": ("L1_xattn_bq", lambda a: np.tile(a.reshape(G, 32).T, (4, 1))),
    "HWqT": ("L1_xattn_Wq", lambda a: a.T), "Hbq": ("L1_xattn_bq", lambda a: a[:, None]),
    "HWkT": ("L1_xattn_Wk", lambda a: a.T), "Hbk": ("L1_xattn_bk", lambda a: a[:, None]), "HWvT": ("L1_xattn_Wv", lambda a: a.T),
    "Hbv2": ("L1_xattn_bv", lambda a: padded_heads(a[:, None])[:, :, 0].T),
    "HWo0": ("L1_xattn_Wo", lambda a: padded_heads(a.T)[0]), "HWo1": ("L1_xattn_Wo", lambda a: padded_heads(a.T)[1]),
    "Hbo": ("L1_xattn_bo", lambda a: a[:, None]),
    "XWq": ("L0_xattn_Wq", lambda a: a), "XWkT": ("L0_xattn_Wk", lambda a: a.T), "XWv": ("L0_xattn_Wv", lambda a: a),
    "Xbq": ("L0_xattn_bq", lambda a: a[:, None]), "Xbk": ("L0_xattn_bk", lambda a: a[:, None]), "Xbv": ("L0_xattn_bv", lambda a: a[:, None]),
    "rms_w": ("L0_attn_rms_w", lambda a: np.tile(a, H)[:, None]),
}


def layouts(inputs):
    x = {"xT": inputs["x"].reshape(NT, D).T, "consts": constants()[0], "ctx": inputs["ctx_1024"],
         "FWgT": inputs["L0_ffn_Wg"].transpose(0, 2, 1), "FWuT": inputs["L0_ffn_Wu"].transpose(0, 2, 1),
         "FWdT": inputs["L0_ffn_Wd"].transpose(0, 2, 1), "ctxT": inputs["ctx_1024"].transpose(0, 2, 1),
         "Mw1": np.concatenate([inputs["L1_ffn_w1"], inputs["L1_ffn_sw1"][None]]),
         "Mw2": np.concatenate([inputs["L1_ffn_w2"], inputs["L1_ffn_sw2"][None]]),
         "Mb1": np.concatenate([inputs["L1_ffn_b1"], inputs["L1_ffn_sb1"][None]]).reshape(E + 1, FT, 128).transpose(0, 2, 1),
         "Mb2": np.concatenate([inputs["L1_ffn_b2"], inputs["L1_ffn_sb2"][None]])}
    for name, (source, lay) in SMALL.items():
        x[name] = lay(inputs[source])
    return {k: np.ascontiguousarray(v) for k, v in x.items()}


def decoder(nc, d, out, upto=99):
    g = Shared()
    g.nc, g.d, g.small = nc, d, list(SMALL) + ["Mb2"]
    with ExitStack() as ctx:
        g.semaphores = []
        sb = lambda n, s, t=F32: ctx.enter_context(nc.sbuf_tensor(n, s, t))
        g.xt, g.xn = sb("xt", [128, NT]), sb("xn", [128, NT])
        _, at = constants()
        g.consts = sb("constants", [128, sum(w for _, w in at.values())])
        g.c = {k: g.consts[:, a:a + w] for k, (a, w) in at.items()}
        g.w = {n: sb(f"w_{n}", list(d[n].shape)) for n in g.small}
        g.eps_ln, g.eps_rms, g.eps_alpha = sb("eps_ln", [128, 1]), sb("eps_rms", [128, 1]), sb("eps_alpha", [128, 1])
        g.ps = ctx.enter_context(nc.psum_tensor("banks", [128, 8, 512], F32))
        g.bank = lambda k: g.ps[:, k, :]
        g.ct = sb("ct", [E, NT])
        g.ct9_dram = nc.dram_tensor("all_expert_weights", [E + 1, NT], F32).ap()
        g.ct_dram = nc.dram_tensor("expert_weights", [E, NT], F32).ap()
        setup(g)
        stages = [(normalize, "n1"), (retention,), (normalize, "n2"), (context_attention,),
                  (normalize, "n3"), (experts0,), (normalize, "n4"), (causal_attention,),
                  (normalize, "n5"), (head_attention,), (normalize, "n6"), (experts1,)]
        for f, *a in (stages[:upto] if isinstance(upto, int) else stages[upto[0]:upto[1]]):
            f(g, *a)
            if len(g.semaphores) > 70:
                nc.clear_and_free_semaphores(g.semaphores)
                nc.all_engine_barrier()
                g.semaphores = []
        stored = g.semaphore("stored")
        with nc.Block() as block:
            @block.sync
            def _(sp):
                sp.dma_start(out, g.xt[:]).then_inc(stored, 16)
                sp.wait_ge(stored, 16)
                sp.wait_ge(stored, 16)


def kernel(**inputs):
    import concourse.bacc as bacc
    from concourse.bass_utils import run_bass_kernel_spmd

    nc = bacc.Bacc("TRN2", target_bir_lowering=False, num_devices=1)
    arrays = layouts({name: np.asarray(a) for name, a in inputs.items()})
    d = {name: nc.dram_tensor(name, a.shape, mybir.dt.from_np(a.dtype), kind="ExternalInput").ap() for name, a in arrays.items()}
    out = nc.dram_tensor("out", [D, NT], F32, kind="ExternalOutput").ap()
    decoder(nc, d, out)
    result = run_bass_kernel_spmd(nc, [arrays], core_ids=[0])
    return np.ascontiguousarray(result.results[0]["out"].T).reshape(B, L, D)
```
